# Optimizing a Trainium2 kernel written in Bass

```python
import numpy as np
import jax
import jax.numpy as jnp

def _softmax(x, axis=-1):
    return jax.nn.softmax(x, axis=axis)

def _gelu(x):
    return jax.nn.gelu(x, approximate=True)

def _silu(x):
    return jax.nn.silu(x)

def _sigmoid(x):
    return jax.nn.sigmoid(x)

def _layernorm(x, axis=-1, eps=1e-05):
    m = jnp.mean(x, axis=axis, keepdims=True)
    v = jnp.var(x, axis=axis, keepdims=True)
    return (x - m) / jnp.sqrt(v + eps)

def _scatter_add(tgt, idx, src, axis=0):
    return tgt.at[idx].add(src)

def _segment_sum(src, seg, n):
    return jax.ops.segment_sum(src, seg, n)
kernel_name = 'mk_prb_d1_jaxref_r4_b4dbb0'

def setup_inputs(seed: int=0):
    np.random.seed(seed)
    _w = jnp.asarray

    def _L0_attn_setup():
        import jax, jax.numpy as jnp
        import numpy as np
        D_MODEL = 512
        N_HEADS = 16
        N_KV_HEADS = 4
        D_K = D_MODEL // N_HEADS
        N_REP = N_HEADS // N_KV_HEADS
        WINDOW = 128
        RMS_EPS = 1e-08
        ROPE_BASE = 10000.0
        MASK_FILL = -10000.0

        def _rmsnorm(x, w):
            rms = jnp.sqrt(jnp.mean(x * x, axis=-1, keepdims=True) + RMS_EPS)
            return x / rms * w

        def _rope(x, cos, sin):
            B, S, H, dk = x.shape
            xr = x.reshape(B, S, H, dk // 2, 2)
            x1, x2 = (xr[..., 0], xr[..., 1])
            c = cos[None, :, None, :]
            s = sin[None, :, None, :]
            o1 = x1 * c - x2 * s
            o2 = x1 * s + x2 * c
            return jnp.stack([o1, o2], axis=-1).reshape(B, S, H, dk)
        key = jax.random.key(seed)
        ks = jax.random.split(key, 10)
        B, S = (2, 512)
        std = 1.0 / np.sqrt(D_MODEL)
        inp = {'x': jax.random.normal(ks[0], (B, S, D_MODEL), dtype=jnp.float32), 'Wq': jax.random.normal(ks[1], (D_MODEL, D_MODEL), dtype=jnp.float32) * std, 'bq': jnp.zeros((D_MODEL,), dtype=jnp.float32), 'Wk': jax.random.normal(ks[2], (N_KV_HEADS * D_K, D_MODEL), dtype=jnp.float32) * std, 'bk': jnp.zeros((N_KV_HEADS * D_K,), dtype=jnp.float32), 'Wv': jax.random.normal(ks[3], (N_KV_HEADS * D_K, D_MODEL), dtype=jnp.float32) * std, 'bv': jnp.zeros((N_KV_HEADS * D_K,), dtype=jnp.float32), 'Wo': jax.random.normal(ks[4], (D_MODEL, D_MODEL), dtype=jnp.float32) * std, 'bo': jnp.zeros((D_MODEL,), dtype=jnp.float32), 'qn_w': jnp.ones((D_K,), dtype=jnp.float32), 'kn_w': jnp.ones((D_K,), dtype=jnp.float32), 'scale': jnp.asarray(1.0 / np.sqrt(D_K), dtype=jnp.float32)}
        return inp
    _L0_attn_in = _L0_attn_setup()

    def _L0_ffn_setup():
        import jax, jax.numpy as jnp
        import numpy as np
        import math
        N_EMBD = 512
        N_HEAD = 16
        HEAD_DIM = N_EMBD // N_HEAD
        B, T = (2, 512)
        key = jax.random.key(seed)
        k1, k2, k3 = jax.random.split(key, 3)
        x = jax.random.normal(k1, (B, T, N_EMBD), dtype=jnp.float32)
        W_gate = jax.random.normal(k2, (N_HEAD, N_EMBD), dtype=jnp.float32) * 0.02
        W_qkv = jax.random.normal(k3, (3 * N_EMBD, N_EMBD), dtype=jnp.float32) * 0.02
        return {'x': x, 'W_gate': W_gate, 'W_qkv': W_qkv}
    _L0_ffn_in = _L0_ffn_setup()
    _d = {'L0_attn_x': _L0_attn_in['x'], 'L0_attn_Wq': _L0_attn_in['Wq'], 'L0_attn_bq': _L0_attn_in['bq'], 'L0_attn_Wk': _L0_attn_in['Wk'], 'L0_attn_bk': _L0_attn_in['bk'], 'L0_attn_Wv': _L0_attn_in['Wv'], 'L0_attn_bv': _L0_attn_in['bv'], 'L0_attn_Wo': _L0_attn_in['Wo'], 'L0_attn_bo': _L0_attn_in['bo'], 'L0_attn_qn_w': _L0_attn_in['qn_w'], 'L0_attn_kn_w': _L0_attn_in['kn_w'], 'L0_attn_scale': _L0_attn_in['scale'], 'L0_ffn_W_gate': _L0_ffn_in['W_gate'], 'L0_ffn_W_qkv': _L0_ffn_in['W_qkv']}
    _x0 = _d['L0_attn_x']
    _d['L0_attn_x'] = jax.random.normal(jax.random.fold_in(jax.random.key(seed), 1), (2, 1024, 512), dtype=_x0.dtype)
    del _x0
    return _d

def reference(L0_attn_x, L0_attn_Wq, L0_attn_bq, L0_attn_Wk, L0_attn_bk, L0_attn_Wv, L0_attn_bv, L0_attn_Wo, L0_attn_bo, L0_attn_qn_w, L0_attn_kn_w, L0_attn_scale, L0_ffn_W_gate, L0_ffn_W_qkv):

    def _L0_attn_ref(x, Wq, bq, Wk, bk, Wv, bv, Wo, bo, qn_w, kn_w, scale):
        import jax, jax.numpy as jnp
        import numpy as np
        D_MODEL = 512
        N_HEADS = 16
        N_KV_HEADS = 4
        D_K = D_MODEL // N_HEADS
        N_REP = N_HEADS // N_KV_HEADS
        WINDOW = 128
        RMS_EPS = 1e-08
        ROPE_BASE = 10000.0
        MASK_FILL = -10000.0

        def _rmsnorm(x, w):
            rms = jnp.sqrt(jnp.mean(x * x, axis=-1, keepdims=True) + RMS_EPS)
            return x / rms * w

        def _rope(x, cos, sin):
            B, S, H, dk = x.shape
            xr = x.reshape(B, S, H, dk // 2, 2)
            x1, x2 = (xr[..., 0], xr[..., 1])
            c = cos[None, :, None, :]
            s = sin[None, :, None, :]
            o1 = x1 * c - x2 * s
            o2 = x1 * s + x2 * c
            return jnp.stack([o1, o2], axis=-1).reshape(B, S, H, dk)
        B, S, D = x.shape
        q = (x @ Wq.T + bq).reshape(B, S, N_HEADS, D_K)
        k = (x @ Wk.T + bk).reshape(B, S, N_KV_HEADS, D_K)
        v = (x @ Wv.T + bv).reshape(B, S, N_KV_HEADS, D_K)
        q = _rmsnorm(q, qn_w)
        k = _rmsnorm(k, kn_w)
        inv_freq = 1.0 / ROPE_BASE ** (jnp.arange(0, D_K, 2, dtype=jnp.float32) / D_K)
        t = jnp.arange(S, dtype=jnp.float32)
        freqs = t[:, None] * inv_freq[None, :]
        cos, sin = (jnp.cos(freqs), jnp.sin(freqs))
        q = _rope(q, cos, sin)
        k = _rope(k, cos, sin)
        q = q.transpose(0, 2, 1, 3)
        k = k.transpose(0, 2, 1, 3)
        v = v.transpose(0, 2, 1, 3)
        k = jnp.repeat(k, N_REP, axis=1)
        v = jnp.repeat(v, N_REP, axis=1)
        scores = jnp.einsum('bhqd,bhkd->bhqk', q, k) * scale
        idx = jnp.arange(S)
        causal = idx[:, None] < idx[None, :]
        local = jnp.abs(idx[:, None] - idx[None, :]) > WINDOW // 2
        mask = causal | local
        scores = jnp.where(mask[None, None, :, :], MASK_FILL, scores)
        attn = jax.nn.softmax(scores, axis=-1)
        out = jnp.einsum('bhqk,bhkd->bhqd', attn, v)
        out = out.transpose(0, 2, 1, 3).reshape(B, S, D)
        return out @ Wo.T + bo

    def _L0_ffn_ref(x, W_gate, W_qkv):
        import jax, jax.numpy as jnp
        import numpy as np
        import math
        N_EMBD = 512
        N_HEAD = 16
        HEAD_DIM = N_EMBD // N_HEAD
        B, T = (2, 512)
        Bb, Tt, C = x.shape
        H, hd = (N_HEAD, HEAD_DIM)
        gating = jax.nn.softmax(x @ W_gate.T, axis=-1)
        idx = jnp.argmax(gating, axis=-1)
        indicator = jax.nn.one_hot(idx, H, dtype=gating.dtype)
        top1_val = jnp.max(gating, axis=-1, keepdims=True)
        gating_top1 = indicator * top1_val
        qkv = x @ W_qkv.T
        q, k, v = jnp.split(qkv, 3, axis=-1)
        k = k.reshape(Bb, Tt, H, hd)
        v = v.reshape(Bb, Tt, H, hd)
        k_shared = jnp.einsum('bth,bthd->btd', indicator, k)
        v_shared = jnp.einsum('bth,bthd->btd', gating_top1, v)
        q = q.reshape(Bb, Tt, H, hd).transpose(0, 2, 1, 3)
        att = jnp.einsum('bhqd,bkd->bhqk', q, k_shared) * (1.0 / math.sqrt(hd))
        causal = jnp.tril(jnp.ones((Tt, Tt), dtype=bool))
        att = jnp.where(causal[None, None, :, :], att, -jnp.inf)
        att = jax.nn.softmax(att, axis=-1)
        y = jnp.einsum('bhqk,bkd->bhqd', att, v_shared)
        y = y.transpose(0, 2, 1, 3).reshape(Bb, Tt, C)
        return y
    x = L0_attn_x
    xn = _layernorm(x, axis=-1)
    x = x + _L0_attn_ref(xn, L0_attn_Wq, L0_attn_bq, L0_attn_Wk, L0_attn_bk, L0_attn_Wv, L0_attn_bv, L0_attn_Wo, L0_attn_bo, L0_attn_qn_w, L0_attn_kn_w, L0_attn_scale) + _L0_ffn_ref(xn, L0_ffn_W_gate, L0_ffn_W_qkv)
    return x

_drawn_inputs = setup_inputs


def setup_inputs(seed=0):
    import zlib

    import numpy as np

    out = dict(_drawn_inputs(seed))
    spreads = {'L0_attn_bq': (0.0, 0.449),
     'L0_attn_bk': (0.0, 0.679),
     'L0_attn_bv': (0.0, 0.1),
     'L0_attn_bo': (0.0, 0.1),
     'L0_attn_qn_w': (1.0, 0.6),
     'L0_attn_kn_w': (1.0, 0.2)}
    factors = {'L0_ffn_W_gate': 3.505}
    for name, (base, spread) in spreads.items():
        noise = np.random.default_rng([zlib.crc32(name.encode()), seed]).standard_normal(out[name].shape)
        drawn = base * np.exp(spread * noise) if base else spread * noise
        out[name] = jnp.asarray(drawn.astype(out[name].dtype))
    for name, factor in factors.items():
        out[name] = (out[name] * factor).astype(out[name].dtype)
    return out
```

```python
import concourse.bass as bass
from concourse import mybir
from contextlib import ExitStack

P = 128
D = 512
KC = D // P
H, HKV, DK = 16, 4, 32
REP = H // HKV
B, S = 2, 1024
TOK = B * S
TILES = TOK // P
PAIR = 2 * P
ROUNDS = TOK // PAIR
HALF = 64
NEG = -1.0e30
LN_EPS, RMS_EPS = 1e-5, 1e-8
HD = H * DK
C_Q, C_KVG, C_FK, C_FV = 0, HD, HD + 2 * HKV * DK + H, 2 * HD + 2 * HKV * DK + H
W_COLS = C_FV + HD
N_QKV = HD + 2 * HKV * DK
KEY0 = 2 * HALF
HALVES = 3 * DK
VW = 64

F32, F32R = mybir.dt.float32, mybir.dt.float32r
ALU, ACT, AX = mybir.AluOpType, mybir.ActivationFunctionType, mybir.AxisListType


class Mark:

    def __init__(self, ctx, nc, book, name, per_round, base):
        self.name, self.per_round, self.sem = name, per_round, ctx.enter_context(nc.semaphore(name))
        self.count, self.at, self.base = 0, {}, base
        book.append(self)

    def by(self, instruction, key=None, inc=1):
        instruction.then_inc(self.sem, inc)
        self.count += inc
        self.at[key] = self.count

    def wait(self, engine, rnd, key=None):
        engine.wait_ge(self.sem, rnd * self.per_round + (self.at[key] + self.base))

    def wait_all(self, engine, rnd):
        if not (isinstance(rnd, int) and rnd * self.per_round + self.count == 0):
            engine.wait_ge(self.sem, rnd * self.per_round + (self.count + self.base))

    def wait_before(self, engine, rnd):
        if not (isinstance(rnd, int) and rnd == 0):
            engine.wait_ge(self.sem, rnd * self.per_round + self.base)


class Stage:

    def __init__(self, ctx, nc, base=1):
        self.ctx, self.nc, self.marks, self.base = ctx, nc, [], base

    def mark(self, name, per_round):
        return Mark(self.ctx, self.nc, self.marks, name, per_round, self.base)

    def prime(self, engine):
        for s in self.marks:
            engine.sem_inc(s.sem, self.base)

    def start(self):
        for s in self.marks:
            s.count = 0

    def end(self):
        wrong = [(s.name, s.per_round, s.count) for s in self.marks if s.count != s.per_round]
        assert not wrong, wrong


def merged(*lists):
    keyed = [((i + 0.5) / len(steps), n, i) for n, steps in enumerate(lists) for i in range(len(steps))]
    return [lists[n][i] for _, n, i in sorted(keyed)]


def mixed_attention_kernel(nc, x, w_tok, w_qt, w_o, b_qkv, b_o, w_norm, scale, rope, ident, rank, out):
    pe, dve, act, pool, sp = nc.tensor, nc.vector, nc.scalar, nc.gpsimd, nc.sync

    q_parts = nc.dram_tensor("q_parts", (2, DK, H, TOK), F32, kind="Internal").ap()
    partial = nc.dram_tensor("partial", (TOK, D), F32, kind="Internal").ap()

    top = ExitStack()

    def sb(ctx, name, shape, dt=F32):
        return ctx.enter_context(nc.sbuf_tensor(name, shape, dt))

    def pb(ctx, name, shape):
        return ctx.enter_context(nc.psum_tensor(name, shape, F32))

    idt = sb(top, "idt", [P, P])
    k_stack = sb(top, "k_stack", [P, TOK], F32R)
    v_all = sb(top, "v_all", [P, TILES, VW])

    one = ExitStack()
    w_tok_p = [sb(one, f"w_tok{n}", [P, KC, W_COLS], F32R) for n in range(2)]
    w_qt_p = [sb(one, f"w_qt{n}", [P, KC, HD], F32R) for n in range(2)]
    w_o_p = [sb(one, f"w_o{n}", [P, KC, D], F32R) for n in range(2)]
    cos_t = sb(one, "cos_t", [P, TILES, 2, DK])
    sin_t = sb(one, "sin_t", [P, TILES, 2, DK])
    bias = sb(one, "bias", [P, N_QKV])
    bias_o = sb(one, "bias_o", [P, D])
    rank_t = sb(one, "rank_t", [P, H])
    win_mask = sb(one, "win_mask", [P, 3 * HALF])
    k_win = sb(one, "k_win", [P, HKV, KEY0 + PAIR], F32R)
    q_win = sb(one, "q_win", [P, H, P], F32R)
    v_nat = [sb(one, f"v_nat{a}", [P, HKV, VW]) for a in range(2)]
    v_shift = [sb(one, f"v_shift{a}", [P, HKV, VW]) for a in range(2)]
    key_bias = sb(one, "key_bias", [P, ROUNDS, HALF])

    setup = Stage(top, nc, base=0)
    raw_used = [setup.mark(f"raw_used{n}", 3) for n in range(2)]
    raw_in = [setup.mark(f"raw_in{n}", 48) for n in range(2)]
    w_hi, const_in, filled, tables = (setup.mark(*a) for a in (
        ("w_hi", 6), ("const_in", 16 * 7), ("filled", 21), ("tables", 5)))
    primed = setup.mark("primed", 1)
    with ExitStack() as ctx:
        raw = [sb(ctx, f"raw{n}", [P, KC, HD]) for n in range(2)]
        rope_t = sb(ctx, "rope_t", [P, TILES, 2, DK])
        norm_w = sb(ctx, "norm_w", [P, 2, 2, DK])
        scale_t = sb(ctx, "scale_t", [P, 1])

        const_in.by(act.dma_start(rope_t[:, :, :, :], rope.rearrange("(t p) a d -> p t a d", p=P)), inc=16)
        for dst, src in ((bias, b_qkv), (bias_o, b_o), (norm_w[:, :, :, :].rearrange("p a b d -> p (a b d)"), w_norm),
                         (scale_t, scale), (rank_t, rank)):
            dst = dst[:, :]
            const_in.by(act.dma_start(dst, src.to_broadcast(dst.shape)), inc=16)
        const_in.by(act.dma_start(idt[:, :], ident), inc=16)

        pieces = [(w_tok, w_tok_p, C_KVG, C_FK - C_KVG), (w_tok, w_tok_p, C_FK, HD), (w_tok, w_tok_p, C_FV, HD),
                  (w_tok, w_tok_p, C_Q, HD), (w_qt, w_qt_p, 0, HD), (w_o, w_o_p, 0, D)]
        for n, (src, dst, c0, cols) in enumerate(pieces):
            buf = n % 2
            raw_used[buf].wait_all(sp, 0)
            raw_in[buf].by(sp.dma_start(raw[buf][:, :, 0:cols],
                                        src[:, c0:c0 + cols].rearrange("(k p) c -> p k c", p=P)), inc=16)
            raw_in[buf].wait(act, 0)
            hi, lo = (d[:, :, c0:c0 + cols] for d in dst)
            w_hi.by(act.activation(hi, raw[buf][:, :, 0:cols], ACT.Copy))
            w_hi.wait(dve, 0)
            raw_used[buf].by(dve.tensor_tensor(lo, raw[buf][:, :, 0:cols], hi.bitcast(F32), ALU.subtract))

        const_in.wait(dve, 0)
        tables.by(dve.tensor_scalar(norm_w[:, :, 0, :], norm_w[:, :, 0, :], scale_t[:, 0:1], None, ALU.mult))
        tables.wait(dve, 0)
        for part, table in ((0, cos_t), (1, sin_t)):
            for who in range(2):
                tables.by(dve.tensor_tensor(
                    table[:, :, who, :], rope_t[:, :, part, :],
                    norm_w[:, part, who, :].unsqueeze(1).to_broadcast([P, TILES, DK]), ALU.mult))

        def fill(instruction):
            filled.by(instruction)
            filled.wait(pool, 0)

        fill(pool.memset(k_stack[96:128, :].bitcast(F32), 1.0))
        fill(pool.memset(k_win[:, :, :].bitcast(F32), 0.0))
        fill(pool.memset(k_win[96:128, :, :].bitcast(F32), 1.0))
        fill(pool.memset(k_win[96:97, :, :].bitcast(F32), 0.0))
        fill(pool.memset(q_win[96:128, :, :].bitcast(F32), 1.0))
        fill(pool.memset(key_bias[96:97, :, :], 0.0))
        for b in range(B):
            fill(pool.memset(key_bias[96:97, b * (S // PAIR):b * (S // PAIR) + 1, :], NEG))
        fill(pool.memset(v_all[:, :, :], 0.0))
        fill(pool.memset(v_all[:, :, DK:DK + 1], 1.0))
        for v in (*v_nat, *v_shift):
            fill(pool.memset(v[:, :, :], 0.0))
            fill(pool.memset(v[:, :, DK:DK + 1], 1.0))
        fill(pool.memset(win_mask[:, :], 0.0))
        for sign in (1, -1):
            fill(pool.affine_select(out=win_mask[:, :], in_=win_mask[:, :], compare_op=ALU.is_ge, fill=NEG,
                                    base=0 if sign == 1 else HALF, pattern=[[sign, 3 * HALF]],
                                    channel_multiplier=-sign))

    NH = H + HKV
    x_ln = sb(one, "x_ln", [P, 2, D])
    x_res = sb(one, "x_res", [P, 2, D])
    xn = [sb(one, f"xn{a}", [P, D]) for a in range(2)]
    stats = sb(one, "stats", [P, 2, 6])
    moments = sb(one, "moments", [P, 2, 2])
    ln_v, ln_y, ln_t, ln_b = (sb(one, n, [P, 2]) for n in ("ln_v", "ln_y", "ln_t", "ln_b"))
    xt = [sb(one, f"xt{n}", [P, KC, PAIR], F32R) for n in range(2)]
    qt = [sb(one, f"qt{n}", [P, 2, PAIR], F32R) for n in range(2)]
    qkv = [sb(one, f"qkv{a}", [P, N_QKV]) for a in range(2)]
    rope_a = sb(one, "rope_a", [P, NH, DK])
    rope_b = sb(one, "rope_b", [P, NH, DK])
    rms_v, rms_y, rms_t = (sb(one, n, [P, NH]) for n in ("rms_v", "rms_y", "rms_t"))
    stack = [sb(one, f"stack{a}", [P, NH, HALVES]) for a in range(2)]
    picked = {k: sb(one, f"picked_{k}", [P, HD]) for k in ("fk", "fv")}
    fk_stack = sb(one, "fk_stack", [P, HALVES])
    g_max, g_sum, g_top, g_rank = (sb(one, n, [P, 2]) for n in ("g_max", "g_sum", "g_top", "g_rank"))
    g_exp, g_score, g_hot = (sb(one, n, [P, 2, H]) for n in ("g_exp", "g_score", "g_hot"))
    w_max = sb(one, "w_max", [P, H])
    w_max_p = sb(one, "w_max_p", [P, 2, H])
    w_max_t = sb(one, "w_max_t", [2 * H, P], F32R)
    p_win = [sb(one, f"p_win{n}", [P, 2, REP, HALF]) for n in range(2)]
    o_win = sb(one, "o_win", [P, 2, REP, 2, HALF])
    recip = sb(one, "recip", [P, 2, REP, 2])
    attn = sb(one, "attn", [P, HD])
    attn_t = [sb(one, f"attn_t{n}", [P, KC, P], F32R) for n in range(2)]

    psum1 = ExitStack()
    gemm = [pb(psum1, f"gemm{n}", [P, 512]) for n in range(2)]
    tp1 = pb(psum1, "tp1", [P, 4, P])
    tp2 = pb(psum1, "tp2", [P, 4, P])
    s_win = [pb(psum1, f"s_win{n}", [P, 2, PAIR]) for n in range(2)]
    st_win = pb(psum1, "st_win", [P, 2, REP, HALF])
    ol = pb(psum1, "ol", [P, 2, REP, HALF])

    st0, st1, st2 = Stage(top, nc), Stage(top, nc), Stage(top, nc)
    x_in, xn_r = st0.mark("x_in", 16), st0.mark("xn_r", 2)
    ln_seq = st0.mark("ln_seq", 8)
    ln_v_r, ln_log, ln_exp, ln_b_r = (st0.mark(n, 1) for n in ("ln_v_r", "ln_log", "ln_exp", "ln_b_r"))
    seq = st1.mark("seq", 26)
    xt_mm, xt_hi, xt_lo = (st1.mark(n, 2) for n in ("xt_mm", "xt_hi", "xt_lo"))
    gemm_mm = [st1.mark(f"gemm_mm{n}", 6) for n in range(2)]
    gemm_read = [st1.mark(f"gemm_read{n}", 6) for n in range(2)]
    kv_r, sq_r, ss_r, rms_log, rms_exp, rms_r = (
        st1.mark(n, 2) for n in ("kv_r", "sq_r", "ss_r", "rms_log", "rms_exp", "rms_r"))
    normed_r, rope_b_r, rope_r, stack_hi, stack_r = (
        st1.mark(n, 2) for n in ("normed_r", "rope_b_r", "rope_r", "stack_hi", "stack_r"))
    g_sum_r, g_top_r = (st1.mark(n, 2) for n in ("g_sum_r", "g_top_r"))
    tree = {k: st1.mark(f"tree_{k}", 8) for k in ("fk", "fv")}
    fk_hi, fk_lo, fk_mm, fk_out, fv_out = (
        st1.mark(n, 2) for n in ("fk_hi", "fk_lo", "fk_mm", "fk_out", "fv_out"))
    fk_dup = st1.mark("fk_dup", 2)
    qt_hi = st1.mark("qt_hi", 4)
    q_stored = [st1.mark(f"q_stored{c}", 64) for c in range(2)]
    v_old, v_r, k_old, k_mm, k_r = (st2.mark(n, k) for n, k in (
        ("v_old", 1), ("v_r", 5), ("k_old", 2), ("k_mm", 2), ("k_r", 2)))
    q_mm, q_r = st2.mark("q_mm", 8), st2.mark("q_r", 8)
    s_mm = [st2.mark(f"s_mm{n}", 8) for n in range(2)]
    s_max = [st2.mark(f"s_max{n}", 16) for n in range(2)]
    w_hi_r, w_lo_r, w_mm, w_t_r, w_in = (st2.mark(n, k) for n, k in (
        ("w_hi_r", 2), ("w_lo_r", 2), ("w_mm", 2), ("w_t_r", 2), ("w_in", 32)))
    st_mm, p_exp = st2.mark("st_mm", 8), st2.mark("p_exp", 8)
    p_low, p_r, pv_mm = ([st2.mark(f"{k}{n}", 4) for n in range(2)] for k in ("p_low", "p_r", "pv_mm"))
    o_r, o_mm, rec_r, attn_r = (st2.mark(n, 4) for n in ("o_r", "o_mm", "rec_r", "attn_r"))
    at_mm, at_hi, at_lo, wo_mm = (st2.mark(n, 2) for n in ("at_mm", "at_hi", "at_lo", "wo_mm"))
    res_in, res_bias, res_r, res_stored = (st2.mark(n, k) for n, k in (
        ("res_in", 16), ("res_bias", 1), ("res_r", 2), ("res_stored", 16)))

    IT = S // P
    HG = HD // P
    HQ = H // HG
    ROUTED_SCALE = float(DK) ** -0.5
    stl, (sta, stb, fin) = [Stage(top, nc) for b in range(B)], (Stage(top, nc) for _ in range(3))
    out_done = [Stage(top, nc) for b in range(B)]
    q_in = [[stl[b].mark(f"q_in{b}{c}", 48) for c in range(4)] for b in range(B)]
    r_in = [stl[b].mark(f"r_in{b}", 16) for b in range(B)]
    rs_mm = [sta.mark(f"rs_mm{n}", 16) for n in range(2)]
    rs_max = [sta.mark(f"rs_max{n}", 16) for n in range(2)]
    r_hi, r_lo, r_mm, r_t, r_row = (sta.mark(n, k) for n, k in (
        ("r_hi", 1), ("r_lo", 1), ("r_mm", 1), ("r_t", 1), ("r_row", 16)))
    rst_mm, rp_exp = ([stb.mark(f"{k}{n}", 18) for n in range(2)] for k in ("rst_mm", "rp_exp"))
    rp_diag, rpv = stb.mark("rp_diag", IT), [stb.mark(f"rpv{n}", 9) for n in range(4)]
    ro_r, ro_mm, ro_rec, ro_norm, ro_out = (stb.mark(n, IT) for n in ("ro_r", "ro_mm", "ro_rec", "ro_norm", "ro_out"))
    stored = [out_done[b].mark(f"stored{b}", 16) for b in range(B)]
    masked = fin.mark("masked", 2)

    for stage in (st0, st1, st2, *stl, sta, stb, fin, *out_done):
        stage.prime(pool)
    primed.by(pool.memset(v_shift[0][:, 0, DK + 1:DK + 2], 0.0))
    for e in (pe, dve, act, pool, sp):
        for s in (*raw_used, tables, filled, const_in, primed):
            s.wait_all(e, 0)
    setup.end()

    def then(signal, instruction, engine, n, alone=False):
        signal.by(instruction, "last")
        signal.wait(engine, n, "last")
        if alone:
            stand_alone(engine)

    def stand_alone(engine):
        engine.nop(nofuse=True)

    def newton(signal, v, y, t, n):
        then(signal, dve.tensor_tensor(t, v, y, ALU.mult), dve, n)
        then(signal, dve.tensor_tensor(t, t, y, ALU.mult), dve, n)
        then(signal, dve.tensor_scalar(t, t, -0.5, 1.5, ALU.mult, ALU.add), dve, n)
        return dve.tensor_tensor(y, y, t, ALU.mult)

    def layernorm(n):
        st0.start()
        xn_r.wait_all(sp, n)
        x_in.by(sp.dma_start(x_ln[:, :, :], x[bass.ds(n * PAIR, PAIR), :].rearrange("(a p) c -> p a c", p=P)), inc=16)
        x_in.wait(dve, n)
        for a in range(2):
            then(ln_seq, dve.bn_stats(stats[:, a, :], x_ln[:, a, :]), dve, n, alone=True)
        for a in range(2):
            then(ln_seq, dve.bn_aggr(moments[:, a, :], stats[:, a, :]), dve, n, alone=True)
        ln_v_r.by(dve.tensor_scalar(ln_v[:, :], moments[:, :, 1], LN_EPS, None, ALU.add))
        ln_v_r.wait(act, n)
        ln_log.by(act.activation(ln_t[:, :], ln_v[:, :], ACT.Ln))
        ln_log.wait(act, n)
        xn_r.wait_all(act, n)
        ln_exp.by(act.activation(ln_y[:, :], ln_t[:, :], ACT.Exp, scale=-0.5))
        ln_exp.wait(dve, n)
        ln_v_r.wait(dve, n)
        then(ln_seq, newton(ln_seq, ln_v[:, :], ln_y[:, :], ln_t[:, :], n), dve, n)
        ln_b_r.by(dve.scalar_tensor_tensor(ln_b[:, :], moments[:, :, 0], -1.0, ln_y[:, :], ALU.mult, ALU.mult))
        ln_b_r.wait(act, n)
        xt_mm.wait_before(act, n)
        for a in range(2):
            xn_r.by(act.activation(xn[a][:, :], x_ln[:, a, :], ACT.Identity, bias=ln_b[:, a:a + 1],
                                   scale=ln_y[:, a:a + 1]), a)
        st0.end()

    def transpose_x(n, a):
        xn_r.wait(pe, n, a)
        xt_lo.wait_all(pe, n)
        fk_out.wait_all(pe, n)
        for kc in range(KC):
            i = pe.transpose(tp1[:, kc, :], xn[a][:, kc * P:(kc + 1) * P], idt[:, :])
        xt_mm.by(i, a)
        cols = slice(a * P, (a + 1) * P)
        if a == 0:
            for g in gemm_mm:
                g.wait_before(act, n)
        xt_mm.wait(act, n, a)
        xt_hi.by(act.activation(xt[0][:, :, cols], tp1[:, :, :], ACT.Copy), a)
        xt_hi.wait(dve, n, a)
        xt_lo.by(dve.tensor_tensor(xt[1][:, :, cols], tp1[:, :, :], xt[0][:, :, cols].bitcast(F32), ALU.subtract), a)

    UNITS = [("kvg", 0), ("fk", 0), ("fv", 0), ("q", 0), ("kvg", 1), ("fk", 1), ("fv", 1), ("qt", 0),
             ("qt", 1), ("q", 1), ("qt", 2), ("qt", 3)]
    COLS = {"q": (C_Q, HD), "kvg": (C_KVG, C_FK - C_KVG), "fk": (C_FK, HD), "fv": (C_FV, HD)}

    def gemm_chunk(n, u, kc):
        (kind, a), bank = UNITS[u], u % 2
        if kc == 0:
            gemm_read[bank].wait_all(pe, n)
            xt_lo.wait(pe, n, 1 if kind == "qt" else a)
        for p, (l, r) in enumerate(((0, 0), (0, 1), (1, 0))):
            first, last = kc == 0 and p == 0, kc == KC - 1 and p == 2
            if kind == "qt":
                i = pe.matmul(gemm[bank][:, 0:PAIR], w_qt_p[r][:, kc, a * P:(a + 1) * P], xt[l][:, kc, :],
                              start=first, stop=last)
            else:
                c0, cols = COLS[kind]
                i = pe.matmul(gemm[bank][:, 0:cols], xt[l][:, kc, a * P:(a + 1) * P],
                              w_tok_p[r][:, kc, c0:c0 + cols], start=first, stop=last)
        if kc == KC - 1:
            gemm_mm[bank].by(i, UNITS[u])
            take = {"q": take_q, "kvg": take_kvg, "fk": take_routed, "fv": take_routed, "qt": take_qt}[kind]
            take(n, kind, a, bank, gemm[bank])

    def take_kvg(n, kind, a, bank, g):
        kv = 2 * HKV * DK
        gate = g[:, kv:kv + H]
        gemm_mm[bank].wait(dve, n, (kind, a))
        v_r.wait_before(dve, n)
        kv_r.by(dve.tensor_tensor(qkv[a][:, HD:N_QKV], g[:, 0:kv], bias[:, HD:N_QKV], ALU.add), a)
        then(seq, dve.tensor_reduce(g_max[:, a:a + 1], gate, AX.X, ALU.max), dve, n)
        then(seq, dve.scalar_tensor_tensor(g_score[:, a, :], gate, g_max[:, a:a + 1], rank_t[:, :],
                                           ALU.is_equal, ALU.mult), dve, n)
        then(seq, dve.tensor_reduce(g_rank[:, a:a + 1], g_score[:, a, :], AX.X, ALU.max), dve, n)
        then(seq, dve.tensor_scalar(g_hot[:, a, :], g_score[:, a, :], g_rank[:, a:a + 1], None, ALU.is_equal), dve, n)
        gemm_read[bank].by(dve.tensor_scalar(g_exp[:, a, :], gate, g_max[:, a:a + 1], None, ALU.subtract))
        gemm_read[bank].wait_all(act, n)
        g_sum_r.by(act.activation(g_exp[:, a, :], g_exp[:, a, :], ACT.Exp, accum_out=g_sum[:, a:a + 1]), a)
        g_sum_r.wait(dve, n, a)
        fv_out.wait_all(dve, n)
        g_top_r.by(dve.reciprocal(g_top[:, a:a + 1], g_sum[:, a:a + 1]), a)

    def take_routed(n, kind, a, bank, g):
        buf = picked[kind]
        gemm_mm[bank].wait(dve, n, (kind, a))
        (fk_dup if kind == "fk" else fv_out).wait_all(dve, n)
        fk_lo.wait_all(dve, n)
        gemm_read[bank].by(dve.tensor_tensor(
            buf[:, :].rearrange("p (h d) -> p h d", h=H), g[:, :].rearrange("p (h d) -> p h d", h=H),
            g_hot[:, a, :].unsqueeze(2).to_broadcast([P, H, DK]), ALU.mult))
        gemm_read[bank].wait_all(pool, n)
        w = HD // 2
        while w >= DK:
            then(tree[kind], pool.tensor_tensor(buf[:, 0:w], buf[:, 0:w], buf[:, w:2 * w], ALU.add), pool, n)
            w //= 2
        tree[kind].wait(act, n, "last")
        if kind == "fv":
            g_top_r.wait(act, n, a)
            fv_out.by(act.activation(v_all[:, bass.ds(2 * n + a, 1), 0:DK], buf[:, 0:DK].unsqueeze(1), ACT.Copy,
                                     scale=g_top[:, a:a + 1]), a)
            return
        fk_mm.wait_all(act, n)
        fk_hi.by(act.activation(fk_stack[:, 0:DK].bitcast(F32R), buf[:, 0:DK], ACT.Copy), a)
        fk_dup.by(act.activation(fk_stack[:, DK:2 * DK].bitcast(F32R), buf[:, 0:DK], ACT.Copy), a)
        fk_dup.wait(dve, n, a)
        fk_lo.by(dve.tensor_tensor(fk_stack[:, 2 * DK:3 * DK].bitcast(F32R), buf[:, 0:DK], fk_stack[:, 0:DK],
                                   ALU.subtract), a)

    def routed_key_stack(n, a):
        fk_lo.wait(pe, n, a)
        xt_lo.wait_all(pe, n)
        fk_out.wait_all(pe, n)
        fk_mm.by(pe.transpose(tp1[0:HALVES, 0, :], fk_stack[:, :], idt[:, :]), a)
        fk_mm.wait(act, n, a)
        fk_out.by(act.activation(k_stack[0:HALVES, bass.ds((2 * n + a) * P, P)], tp1[0:HALVES, 0, :], ACT.Copy), a)

    def take_q(n, kind, a, bank, g):
        gemm_mm[bank].wait(dve, n, (kind, a))
        v_r.wait_before(dve, n)
        gemm_read[bank].by(dve.tensor_tensor(qkv[a][:, 0:HD], g[:, :], bias[:, 0:HD], ALU.add))
        qk = qkv[a][:, 0:NH * DK].rearrange("p (h d) -> p h d", h=NH)
        gemm_read[bank].wait_all(act, n)
        rope_r.wait_all(act, n)
        sq_r.by(act.activation(rope_b[:, :, :], qk, ACT.Square), a)
        sq_r.wait(dve, n, a)
        then(seq, dve.tensor_reduce(rms_t[:, :], rope_b[:, :, :], AX.X, ALU.add), dve, n)
        ss_r.by(dve.tensor_scalar(rms_v[:, :], rms_t[:, :], 1.0 / DK, RMS_EPS, ALU.mult, ALU.add), a)
        ss_r.wait(act, n, a)
        ss_r.wait(dve, n, a)
        rms_log.by(act.activation(rms_t[:, :], rms_v[:, :], ACT.Ln), a)
        rms_log.wait(act, n, a)
        normed_r.wait_all(act, n)
        rms_exp.by(act.activation(rms_y[:, :], rms_t[:, :], ACT.Exp, scale=-0.5), a)
        rms_exp.wait(dve, n, a)
        rms_r.by(newton(seq, rms_v[:, :], rms_y[:, :], rms_t[:, :], n), a)
        rms_r.wait(pool, n, a)
        rope_r.wait_all(pool, n)
        kv_r.wait(pool, n, a)
        normed_r.by(pool.tensor_tensor(qk, qk, rms_y[:, :].unsqueeze(2).to_broadcast([P, NH, DK]),
                                       ALU.mult), a)
        normed_r.wait(pool, n, a)
        normed_r.wait(dve, n, a)
        t = bass.ds(2 * n + a, 1)
        for who, h0, hn in ((1, H, HKV), (0, 0, H)):
            src = qk[:, h0:h0 + hn, :]
            sin_w = sin_t[:, t, who, :].rearrange("p o (s d) -> p o s d", s=2).to_broadcast([P, hn, 2, DK // 2])
            i = pool.tensor_tensor(rope_b[:, h0:h0 + hn, :].rearrange("p h (s d) -> p h s d", s=2),
                                   src.rearrange("p h (s d) -> p h s d", s=2)[:, :, ::-1, :], sin_w, ALU.mult)
            j = dve.tensor_tensor(rope_a[:, h0:h0 + hn, :], src, cos_t[:, t, who, :].to_broadcast([P, hn, DK]), ALU.mult)
            if who:
                seq.by(j)
        rope_b_r.by(i, a)
        then(seq, j, dve, n)
        rope_b_r.wait(dve, n, a)
        rope_r.by(dve.tensor_tensor(rope_a[:, :, :], rope_a[:, :, :], rope_b[:, :, :], ALU.add), a)
        rope_r.wait(act, n, a)
        rope_r.wait(dve, n, a)
        if not (isinstance(n, int) and n == 0):
            q_mm.wait(act, n - 1, (a, HKV - 1))
        st = stack[a]
        stack_hi.by(act.activation(st[:, :, 0:DK].bitcast(F32R), rope_a[:, :, :], ACT.Copy), a)
        stack_hi.wait(dve, n, a)
        for h0, h1, lo, dup in ((0, H, 1, 2), (H, NH, 2, 1)):
            seq.by(dve.tensor_copy(st[:, h0:h1, dup * DK:(dup + 1) * DK], st[:, h0:h1, 0:DK]))
            i = dve.tensor_tensor(st[:, h0:h1, lo * DK:(lo + 1) * DK].bitcast(F32R), rope_a[:, h0:h1, :],
                                  st[:, h0:h1, 0:DK], ALU.subtract)
            (stack_r if h0 else seq).by(i, a)

    def take_qt(n, kind, c, bank, g):
        q_stored[c % 2].wait_all(act, n)
        gemm_mm[bank].wait(act, n, (kind, c))
        qt_hi.by(act.activation(qt[0][:, c % 2, :], g[:, 0:PAIR], ACT.Copy), c)
        qt_hi.wait(dve, n, c)
        i = dve.tensor_tensor(qt[1][:, c % 2, :], g[:, 0:PAIR], qt[0][:, c % 2, :].bitcast(F32), ALU.subtract)
        gemm_read[bank].by(i)
        gemm_read[bank].wait_all(sp, n)
        for part in range(2):
            dst = q_parts[part, :, 4 * c:4 * c + 4, bass.ds(n * PAIR, PAIR)].rearrange("d h t -> h d t")
            q_stored[c % 2].by(sp.dma_start(dst, qt[part][:, c % 2, :].bitcast(F32)), inc=16)

    def stage1(n):
        first = [lambda a=a: transpose_x(n, a) for a in range(2)]
        steps = []
        for u, (kind, a) in enumerate(UNITS):
            for kc in range(KC):
                steps.append(lambda u=u, kc=kc: gemm_chunk(n, u, kc))
                if kc == 3 and kind == "kvg" and a == 1:
                    steps.append(lambda: routed_key_stack(n, 0))
                if kc == 3 and kind == "q" and a == 1:
                    steps.append(lambda: routed_key_stack(n, 1))
        return first, steps

    def load_old(m):
        kk = k_win[0:HALVES, :, HALF:KEY0]
        for s in pv_mm:
            s.wait_all(act, m)
        v_old.by(act.activation(v_shift[0][0:HALF, :, 0:DK], v_nat[1][HALF:P, :, 0:DK], ACT.Copy))
        k_old.by(act.activation(kk, k_win[0:HALVES, :, PAIR + HALF:PAIR + KEY0].bitcast(F32), ACT.Copy))
        k_old.by(act.activation(k_win[96:97, :, HALF:KEY0], key_bias[96:97, bass.ds(m, 1), :].to_broadcast(
            [1, HKV, HALF]), ACT.Copy))
        v_old.wait(act, m)
        kv_r.wait(act, m, 1)
        val = [qkv[a][:, NH * DK:].rearrange("p (g d) -> p g d", g=HKV) for a in range(2)]
        v_r.by(act.activation(v_shift[1][0:HALF, :, 0:DK], val[0][HALF:P], ACT.Copy))
        for a in range(2):
            v_r.by(act.activation(v_shift[a][HALF:P, :, 0:DK], val[a][0:HALF], ACT.Copy))
            v_r.by(act.activation(v_nat[a][:, :, 0:DK], val[a], ACT.Copy))

    def load_res(m):
        res_stored.wait_all(sp, m)
        res_in.by(sp.dma_start(x_res[:, :, :], x[bass.ds(m * PAIR, PAIR), :].rearrange("(a p) c -> p a c", p=P)), inc=16)
        res_in.wait(pool, m)
        res_bias.by(pool.tensor_tensor(x_res[:, :, :], x_res[:, :, :],
                                       bias_o[:, :].unsqueeze(1).to_broadcast([P, 2, D]), ALU.add))

    def tp2_free(m):
        for s in (k_r, q_r, w_t_r, at_lo):
            s.wait_all(pe, m)

    def key_stack(m, a):
        stack_r.wait(pe, m, a)
        tp2_free(m)
        for g in range(HKV):
            i = pe.transpose(tp2[0:HALVES, g, :], stack[a][:, H + g, :], idt[:, :])
        k_mm.by(i, a)
        k_mm.wait(act, m, a)
        k_old.wait(act, m)
        k_r.by(act.activation(k_win[0:HALVES, :, KEY0 + a * P:KEY0 + (a + 1) * P], tp2[0:HALVES, :, :], ACT.Copy), a)

    def query_stack(m, a, g):
        stack_r.wait(pe, m, a)
        tp2_free(m)
        for h in range(REP):
            i = pe.transpose(tp2[0:HALVES, h, :], stack[a][:, REP * g + h, :], idt[:, :])
        q_mm.by(i, (a, g))
        q_mm.wait(act, m, (a, g))
        st_mm.wait_all(act, m)
        q_r.by(act.activation(q_win[0:HALVES, REP * g:REP * g + REP, :], tp2[0:HALVES, :, :], ACT.Copy), (a, g))

    def s_win_free(m, n):
        s_max[n].wait_all(pe, m)
        attn_r.wait_all(pe, m)
        res_r.wait_all(pe, m)

    def scores(m, a, g, pair):
        n = pair
        q_r.wait(pe, m, (a, g))
        k_r.wait(pe, m, a)
        s_win_free(m, n)
        for k in range(2):
            h = REP * g + 2 * pair + k
            i = pe.matmul(s_win[n][:, k, :], q_win[0:HALVES + 1, h, :], k_win[0:HALVES + 1, g, a * P:a * P + PAIR],
                          start=True, stop=True)
        s_mm[n].by(i, (a, g))
        s_mm[n].wait(dve, m, (a, g))
        if g == 0 and pair == 0:
            w_lo_r.wait_all(dve, m)
        stand_alone(dve)
        for k in range(2):
            h = REP * g + 2 * pair + k
            s_max[n].by(dve.tensor_tensor_reduce(
                out=s_win[n][:, k, HALF:PAIR], in0=s_win[n][:, k, HALF:PAIR], in1=win_mask[:, :], scale=1.0,
                scalar=NEG, op0=ALU.add, op1=ALU.max, accum_out=w_max[:, h:h + 1]), (a, g))

    def maxima(m, a):
        w_mm.wait_all(dve, m)
        for s in s_max:
            s.wait(dve, m, (a, HKV - 1))
        w_hi_r.by(dve.tensor_scalar(w_max_p[:, 0, :].bitcast(F32R), w_max[:, :], -1.0, None, ALU.mult), a)
        w_hi_r.wait(dve, m, a)
        w_lo_r.by(dve.scalar_tensor_tensor(w_max_p[:, 1, :].bitcast(F32R), w_max[:, :], -1.0, w_max_p[:, 0, :],
                                           ALU.mult, ALU.subtract), a)

    def maxima_rows(m, a):
        w_lo_r.wait(pe, m, a)
        tp2_free(m)
        w_mm.by(pe.transpose(tp2[0:2 * H, 0, :], w_max_p[:, :, :].rearrange("p s h -> p (s h)"), idt[:, :]), a)
        w_in.wait_all(act, m)
        w_mm.wait(act, m, a)
        w_t_r.by(act.activation(w_max_t[:, :], tp2[0:2 * H, 0, :], ACT.Copy), a)
        w_t_r.wait(sp, m, a)
        w_in.by(sp.dma_start(q_win[HALVES + 1:HALVES + 3, :, :].bitcast(F32),
                             w_max_t[:, :].bitcast(F32)), a, inc=16)

    def weights(m, a, blk, kvp):
        n = kvp
        w_in.wait(pe, m, a)
        q_r.wait(pe, m, (a, HKV - 1))
        p_exp.wait_all(pe, m)
        w0 = HALF + a * P + blk * HALF
        for c in range(2):
            g = 2 * kvp + c
            i = pe.matmul(st_win[:, c, :, :], k_win[0:HALVES + 3, g, w0:w0 + P],
                          q_win[0:HALVES + 3, REP * g:REP * g + REP, blk * HALF:(blk + 1) * HALF], start=True, stop=True)
        st_mm.by(i, (a, blk, kvp))
        st_mm.wait(act, m, (a, blk, kvp))
        pv_mm[n].wait_all(act, m)
        p_exp.by(act.activation(p_win[n][:, :, :, :], st_win[:, :, :, :], ACT.Exp), (a, blk, kvp))
        p_exp.wait(pool, m, (a, blk, kvp))
        stand_alone(pool)
        for sign, s in ((1, p_low[n]), (-1, p_r[n])):
            s.by(pool.affine_select(out=p_win[n][:, :, :, :], in_=p_win[n][:, :, :, :], compare_op=ALU.is_ge, fill=0.0,
                                    base=0 if sign == 1 else HALF, pattern=[[0, 2], [0, REP], [-sign, HALF]],
                                    channel_multiplier=sign), (a, blk))
            s.wait(pool, m, (a, blk))
            stand_alone(pool)

    def values(m, a, blk, kvp):
        n = kvp
        p_r[n].wait(pe, m, (a, blk))
        v_r.wait(pe, m)
        if kvp == 0:
            o_r.wait_all(pe, m)
        v = (v_nat if blk else v_shift)[a]
        for c in range(2):
            i = pe.matmul(ol[c * VW:(c + 1) * VW, kvp, :, :], v[:, 2 * kvp + c, :], p_win[n][:, c, :, :],
                          start=True, stop=True)
        pv_mm[n].by(i, (a, blk))
        if kvp == 1:
            pv_mm[n].wait(act, m, (a, blk))
            o_mm.wait_all(act, m)
            o_r.by(act.activation(o_win[:, :, :, blk, :], ol[:, :, :, :], ACT.Copy), (a, blk))

    def normalise(m, a, kvp):
        o_r.wait(pe, m, (a, 1))
        s_win_free(m, kvp)
        for h in range(REP):
            i = pe.transpose(s_win[kvp][:, :, :].rearrange("p a (b c) -> p (a b) c", b=2)[:, h, :],
                             o_win[:, kvp, h, :, :].rearrange("p b q -> p (b q)"), idt[:, :])
        o_mm.by(i, (a, kvp))
        o_mm.wait(dve, m, (a, kvp))
        src = s_win[kvp][:, :, :].rearrange("p a b -> p (a b)").rearrange("p (h c v) -> p h c v", h=REP, c=2)
        rec_r.by(dve.reciprocal(recip[:, kvp, :, :], src[:, :, :, DK]), (a, kvp))
        rec_r.wait(dve, m, (a, kvp))
        at_mm.wait_all(dve, m)
        dst = attn[:, kvp * 2 * REP * DK:(kvp + 1) * 2 * REP * DK].rearrange("p (c h d) -> p h c d", c=2, h=REP)
        attn_r.by(dve.tensor_tensor(dst, src[:, :, :, 0:DK],
                                    recip[:, kvp, :, :].unsqueeze(3).to_broadcast([P, REP, 2, DK]), ALU.mult), (a, kvp))

    def attn_transposed(m, a):
        attn_r.wait(pe, m, (a, 1))
        tp2_free(m)
        for kc in range(KC):
            i = pe.transpose(tp2[:, kc, :], attn[:, kc * P:(kc + 1) * P], idt[:, :])
        at_mm.by(i, a)
        at_mm.wait(act, m, a)
        wo_mm.wait_all(act, m)
        at_hi.by(act.activation(attn_t[0][:, :, :], tp2[:, :, :], ACT.Copy), a)
        at_hi.wait(dve, m, a)
        at_lo.by(dve.tensor_tensor(attn_t[1][:, :, :], tp2[:, :, :], attn_t[0][:, :, :].bitcast(F32), ALU.subtract), a)

    def out_projection(m, a, kc):
        wo = s_win[0][:, :, :].rearrange("p a b -> p (a b)")
        if kc == 0:
            at_lo.wait(pe, m, a)
            s_win_free(m, 0)
        for p, (l, r) in enumerate(((0, 0), (0, 1), (1, 0))):
            i = pe.matmul(wo, attn_t[l][:, kc, :], w_o_p[r][:, kc, :], start=kc == 0 and p == 0,
                          stop=kc == KC - 1 and p == 2)
        if kc < KC - 1:
            return
        wo_mm.by(i, a)
        wo_mm.wait(dve, m, a)
        res_bias.wait(dve, m)
        res_r.by(dve.tensor_tensor(x_res[:, a, :], wo, x_res[:, a, :], ALU.add), a)
        if a == 1:
            res_r.wait(sp, m, a)
            res_stored.by(sp.dma_start(partial[bass.ds(m * PAIR, PAIR), :].rearrange("(a p) c -> p a c", p=P),
                                       x_res[:, :, :]), inc=16)

    def stage2(m):
        first = [lambda: load_old(m), lambda: load_res(m)]
        steps = []
        for a in range(2):
            steps.append(lambda a=a: key_stack(m, a))
            for g in range(HKV):
                steps.append(lambda a=a, g=g: query_stack(m, a, g))
                if g:
                    steps += [lambda a=a, g=g - 1, k=k: scores(m, a, g, k) for k in range(2)]
            steps += [lambda a=a, k=k: scores(m, a, HKV - 1, k) for k in range(2)]
            steps.append(lambda a=a: maxima(m, a))
            steps.append(lambda a=a: maxima_rows(m, a))
            last = None
            for blk in range(2):
                for kvp in range(2):
                    steps.append(lambda a=a, b=blk, k=kvp: weights(m, a, b, k))
                    if last:
                        steps.append(last)
                    last = lambda a=a, b=blk, k=kvp: values(m, a, b, k)
            steps.append(last)
            steps += [lambda a=a, k=k: normalise(m, a, k) for k in range(2)]
            steps.append(lambda a=a: attn_transposed(m, a))
            steps += [lambda a=a, kc=kc: out_projection(m, a, kc) for kc in range(KC)]
        return first, steps

    def body(n, project, attend, norm):
        first1, steps1 = stage1(n) if project else ([], [])
        first2, steps2 = stage2(n - 1) if attend else ([], [])
        if project:
            st1.start()
        if attend:
            st2.start()
        steps = merged(*[s for s in (steps1, steps2, [lambda: layernorm(n + 1)] if norm else []) if s])
        for step in first1 + first2 + steps:
            step()
        if project:
            st1.end()
        if attend:
            st2.end()

    layernorm(0)
    body(0, True, False, True)
    with nc.Fori(1, ROUNDS - 1, 1) as n:
        body(n, True, True, True)
    body(ROUNDS - 1, True, True, False)
    body(ROUNDS, False, True, False)
    for e in (pe, dve, act, pool, sp):
        for s in (*q_stored, *gemm_read, fk_out, fv_out, stack_r):
            s.wait_before(e, ROUNDS)
        for s in (res_stored, res_r, *p_r, o_r):
            s.wait_before(e, ROUNDS)
    psum1.close()
    one.close()

    two = ExitStack()
    q_op = [sb(two, f"q_op{b}", [P, HQ, S], F32R) for b in range(B)]
    p_t = [sb(two, f"p_t{n}", [P, HQ, P]) for n in range(4)]
    causal = sb(two, "causal", [P, S])
    r_max = sb(two, "r_max", [P, HQ, IT])
    r_max_p = sb(two, "r_max_p", [P, 2, HQ, IT])
    r_max_t = sb(two, "r_max_t", [2 * HQ * IT, P], F32R)
    o_sb = [sb(two, f"o_sb{n}", [P, 2, P]) for n in range(2)]
    o_rec = sb(two, "o_rec", [P, 2, 2])
    o_norm = sb(two, "o_norm", [P, P])
    res = [sb(two, f"res{b}", [P, IT, P]) for b in range(B)]
    out_sb = [sb(two, f"out_sb{b}", [P, IT, P]) for b in range(B)]
    s_ps = [pb(two, f"s_ps{n}", [P, S]) for n in range(2)]
    st_ps = [pb(two, f"st_ps{n}", [P, HQ, P]) for n in range(2)]
    o_ps = pb(two, "o_ps", [P, 2, P])
    tp_ps = pb(two, "tp_ps", [P, 4, P])

    masked.by(pool.memset(causal[:, :], 0.0))
    masked.wait(pool, 0)
    masked.by(pool.affine_select(out=causal[:, S - P:S], in_=causal[:, S - P:S], compare_op=ALU.is_ge, fill=NEG,
                                 base=0, pattern=[[-1, P]], channel_multiplier=1))
    masked.wait(dve, 0)

    def load_queries(u, hg, b, c):
        t = slice(c * PAIR, (c + 1) * PAIR)
        for blk, part in ((0, 0), (1, 1), (2, 0)):
            q_in[b][c].by(sp.dma_start(
                q_op[b][blk * DK:(blk + 1) * DK, :, t].bitcast(F32),
                q_parts[part, :, bass.ds(hg * HQ, HQ), b * S + c * PAIR:b * S + (c + 1) * PAIR]), inc=16)

    def load_partial(u, hg, b):
        r_in[b].by(sp.dma_start(res[b][:, :, :], partial[b * S:(b + 1) * S, bass.ds(hg * P, P)].rearrange(
            "(i p) c -> p i c", p=P)), inc=16)

    def row_scores(u, hg, b, i, h):
        n = h % 2
        q_in[b][i // 2].wait_before(pe, hg + 1)
        rs_max[n].wait_all(pe, u)
        width = (i + 1) * P
        for c0 in range(0, width, 512):
            cols = max(min(width - c0, 512), 2 * P)
            m = pe.matmul(s_ps[n][:, c0:c0 + cols], q_op[b][0:HALVES, h, i * P:(i + 1) * P],
                          k_stack[0:HALVES, b * S + c0:b * S + c0 + cols], start=True, stop=True)
        rs_mm[n].by(m, (i, h))
        rs_mm[n].wait(dve, u, (i, h))
        if i == 0 and h == 0:
            r_lo.wait_all(dve, u)
        stand_alone(dve)
        rs_max[n].by(dve.tensor_tensor_reduce(
            out=s_ps[n][:, 0:width], in0=s_ps[n][:, 0:width], in1=causal[:, S - width:S], scale=1.0, scalar=NEG,
            op0=ALU.add, op1=ALU.max, accum_out=r_max[:, h, i:i + 1]), (i, h))

    def row_maxima(u, b):
        r_mm.wait_all(dve, u)
        for s in rs_max:
            s.wait_all(dve, u)
        r_hi.by(dve.tensor_scalar(r_max_p[:, 0, :, :].bitcast(F32R), r_max[:, :, :], -1.0, None, ALU.mult))
        r_hi.wait(dve, u)
        r_lo.by(dve.scalar_tensor_tensor(r_max_p[:, 1, :, :].bitcast(F32R), r_max[:, :, :], -1.0, r_max_p[:, 0, :, :],
                                         ALU.mult, ALU.subtract))

    def tp_ps_free(u_a, u_b):
        if u_a is None:
            r_t.wait_before(pe, u_b + 1)
            ro_norm.wait_all(pe, u_b)
        else:
            r_t.wait_all(pe, u_a)
            ro_norm.wait_all(pe, u_b) if u_b is not None else None

    def maxima_into_rows(u, b, u_b):
        r_lo.wait(pe, u)
        if u_b is not None:
            ro_norm.wait_all(pe, u_b)
        r_t.wait_all(pe, u)
        stand_alone(pe)
        r_mm.by(pe.transpose(tp_ps[0:2 * HQ * IT, 0, :], r_max_p[:, :, :, :].rearrange("p s h i -> p (s h i)"), idt[:, :]))
        r_mm.wait(act, u)
        r_row.wait_all(act, u)
        r_t.by(act.activation(r_max_t[:, :], tp_ps[0:2 * HQ * IT, 0, :], ACT.Copy))
        r_t.wait(act, u)
        r_row.by(act.dma_start(q_op[b][HALVES:HALVES + 2, :, :].bitcast(F32),
                               r_max_t[:, :].bitcast(F32)), inc=16)

    def key_scores(u, b, k, i, j):
        n, r = k % 2, k % 4
        if k == 0:
            r_row.wait_before(pe, u + 1)
        rp_exp[n].wait_all(pe, u)
        rst_mm[n].by(pe.matmul(st_ps[n][:, :, :], k_stack[0:HALVES + 2, b * S + j * P:b * S + (j + 1) * P],
                               q_op[b][0:HALVES + 2, :, i * P:(i + 1) * P], start=True, stop=True), k)
        rst_mm[n].wait(act, u, k)
        rpv[r].wait_all(act, u)
        rp_exp[n].by(act.activation(p_t[r][:, :, :], st_ps[n][:, :, :], ACT.Exp, scale=ROUTED_SCALE), k)
        if i == j:
            rp_exp[n].wait(pool, u, k)
            stand_alone(pool)
            rp_diag.by(pool.affine_select(out=p_t[r][:, :, :], in_=p_t[r][:, :, :], compare_op=ALU.is_ge, fill=0.0,
                                          base=0, pattern=[[0, HQ], [1, P]], channel_multiplier=-1), i)

    def weighted_values(u, b, k, i, j):
        n, r = k % 2, k % 4
        rp_exp[n].wait(pe, u, k)
        if i == j:
            rp_diag.wait(pe, u, i)
        if j == 0:
            ro_r.wait_all(pe, u)
        for c in range(2):
            m = pe.matmul(o_ps[c * VW:(c + 1) * VW, :, :], v_all[:, b * IT + j, :], p_t[r][:, 2 * c:2 * c + 2, :],
                          start=j == 0, stop=j == i)
        rpv[r].by(m, k)
        if i == j:
            rpv[r].wait(act, u, k)
            ro_mm.wait_all(act, u)
            ro_r.by(act.activation(o_sb[i % 2][:, :, :], o_ps[:, :, :], ACT.Copy), i)

    def finish_rows(u, hg, b, i):
        ro_r.wait(pe, u, i)
        ro_norm.wait_all(pe, u)
        if maxima_round[0] is not None:
            r_t.wait_before(pe, maxima_round[0])
        for h in range(2):
            m = pe.transpose(tp_ps[:, h, :], o_sb[i % 2][:, h, :], idt[:, :])
        ro_mm.by(m, i)
        ro_mm.wait(dve, u, i)
        src = tp_ps[:, 0:2, :].rearrange("p h (c v) -> p h c v", c=2)
        ro_rec.by(dve.reciprocal(o_rec[:, :, :], src[:, :, :, DK]), i)
        ro_rec.wait(dve, u, i)
        ro_norm.by(dve.tensor_tensor(o_norm[:, :].rearrange("p (c h d) -> p h c d", c=2, h=2), src[:, :, :, 0:DK],
                                     o_rec[:, :, :].unsqueeze(3).to_broadcast([P, 2, 2, DK]), ALU.mult), i)
        ro_norm.wait(dve, u, i)
        if i == 0:
            r_in[b].wait_before(dve, hg + 1)
            stored[b].wait_before(dve, hg)
        ro_out.by(dve.tensor_tensor(out_sb[b][:, i, :], o_norm[:, :], res[b][:, i, :], ALU.add), i)

    def store(u, hg, b):
        ro_out.wait_all(sp, u)
        stored[b].by(sp.dma_start(out[b * S:(b + 1) * S, bass.ds(hg * P, P)].rearrange("(i p) c -> p i c", p=P),
                               out_sb[b][:, :, :]), inc=16)

    maxima_round = [None]

    def phase(now, before, ahead):
        a_steps, b_steps = [], []
        if now:
            u, hg, b = now
            sta.start()
            a_steps = [lambda i=i, h=h: row_scores(u, hg, b, i, h) for i in range(IT) for h in range(HQ)]

            def rows():
                row_maxima(u, b)

            def into_rows():
                maxima_into_rows(u, b, before and before[0])
                maxima_round[0] = u + 1

            a_steps += [rows, into_rows]
            a_steps += [lambda: None] * (6 if before else 0)
            maxima_round[0] = u
        if before:
            bu, bhg, bb = before
            stb.start()
            if not now:
                maxima_round[0] = bu + 1
            if ahead:
                stl[bb].start()
            steps = [(i, j) for i in range(IT) for j in range(i + 1)]
            done = []
            for k, (i, j) in enumerate(steps + [None, None, None, None]) if False else []:
                pass
            for k in range(len(steps) + 4):
                if k < len(steps):
                    b_steps.append(lambda k=k: key_scores(bu, bb, k, *steps[k]))
                if 2 <= k < len(steps) + 2:
                    b_steps.append(lambda k=k - 2: weighted_values(bu, bb, k, *steps[k]))
                if 4 <= k and steps[k - 4][0] == steps[k - 4][1]:
                    i = steps[k - 4][0]
                    b_steps.append(lambda i=i: finish_rows(bu, bhg, bb, i))
                    if ahead and i % 2:
                        def load(c=i // 2):
                            for s in rst_mm:
                                s.wait_all(sp, bu)
                                stand_alone(sp)
                            load_queries(*ahead, c)
                        b_steps.append(load)
            def last():
                store(bu, bhg, bb)
                if ahead:
                    load_partial(*ahead)
            b_steps.append(last)
        for step in merged(*[s for s in (b_steps, a_steps) if s]):
            step()
        if now:
            sta.end()
        if before:
            stb.end()
            if ahead:
                stl[bb].end()

    for b in range(B):
        stl[b].start()
        for c in range(4):
            load_queries(b, 0, b, c)
        load_partial(b, 0, b)
        stl[b].end()
    phase((0, 0, 0), None, None)
    with nc.Fori(0, HG - 1, 1) as hg:
        phase((2 * hg + 1, hg, 1), (2 * hg, hg, 0), (2 * hg + 2, hg + 1, 0))
        phase((2 * hg + 2, hg + 1, 0), (2 * hg + 1, hg, 1), (2 * hg + 3, hg + 1, 1))
    g = HG - 1
    phase((2 * g + 1, g, 1), (2 * g, g, 0), None)
    phase(None, (2 * g + 1, g, 1), None)
    for b in range(B):
        stored[b].wait_before(sp, HG)
    two.close()
    top.close()


def rope_table():
    import numpy as np
    inv = (np.float32(1.0) / np.float32(10000.0) ** (np.arange(0, DK, 2, dtype=np.float32) / np.float32(DK)))
    f = np.arange(S, dtype=np.float32)[:, None] * inv.astype(np.float32)[None, :]
    c, s = np.cos(f), np.sin(f)
    t = np.stack([np.concatenate([c, c], 1), np.concatenate([-s, s], 1)], 1).astype(np.float32)
    return np.concatenate([t] * B, 0)


def kernel(**inputs):
    import numpy as np
    import concourse.bacc as bacc
    from concourse.bass_utils import run_bass_kernel_spmd

    a = {k: np.asarray(v) for k, v in inputs.items()}
    even_first = np.concatenate([np.arange(0, DK, 2), np.arange(1, DK, 2)])
    odd_first = np.concatenate([np.arange(1, DK, 2), np.arange(0, DK, 2)])

    def heads(w):
        return w.reshape(-1, DK, *w.shape[1:])[:, even_first].reshape(w.shape)

    wq, wk = heads(a["L0_attn_Wq"]), heads(a["L0_attn_Wk"])
    fq, fk, fv = np.split(a["L0_ffn_W_qkv"], 3, axis=0)
    qn, kn = a["L0_attn_qn_w"], a["L0_attn_kn_w"]
    arrays = {
        "x": a["L0_attn_x"].reshape(TOK, D),
        "w_tok": np.concatenate([wq, wk, a["L0_attn_Wv"], a["L0_ffn_W_gate"], fk, fv], 0).T,
        "w_qt": fq.T,
        "w_o": a["L0_attn_Wo"].T,
        "b_qkv": np.concatenate([heads(a["L0_attn_bq"]), heads(a["L0_attn_bk"]), a["L0_attn_bv"]])[None, :],
        "b_o": a["L0_attn_bo"][None, :],
        "w_norm": np.concatenate([qn[even_first], kn[even_first], qn[odd_first], kn[odd_first]])[None, :],
        "scale": a["L0_attn_scale"].reshape(1, 1),
        "rope": rope_table(),
        "ident": np.eye(P, dtype=np.float32),
        "rank": (H - np.arange(H, dtype=np.float32))[None, :],
    }
    arrays = {k: np.ascontiguousarray(v) for k, v in arrays.items()}
    nc = bacc.Bacc("TRN2", target_bir_lowering=False, num_devices=1)
    args = [nc.dram_tensor(k, v.shape, mybir.dt.from_np(v.dtype), kind="ExternalInput").ap() for k, v in arrays.items()]
    out = nc.dram_tensor("out", (TOK, D), F32, kind="ExternalOutput").ap()
    mixed_attention_kernel(nc, *args, out)
    r = run_bass_kernel_spmd(nc, [arrays], core_ids=[0])
    return r.results[0]["out"].reshape(B, S, D)
```

```python
import concourse.bass as bass
from concourse import mybir
from collections import deque
from contextlib import ExitStack

P = 128
D = 512
KC = D // P
H, HKV, DK = 16, 4, 32
REP = H // HKV
B, S = 2, 1024
TOK = B * S
TILES = TOK // P
PAIR = 2 * P
ROUNDS = TOK // PAIR
HALF = 64
NEG = -1.0e30
LN_EPS, RMS_EPS = 1e-5, 1e-8
HD = H * DK
C_Q, C_KVG, C_FK, C_FV = 0, HD, HD + 2 * HKV * DK + H, 2 * HD + 2 * HKV * DK + H
W_COLS = C_FV + HD
N_QKV = HD + 2 * HKV * DK
KEY0 = 2 * HALF
HALVES = 3 * DK
VW = 64

F32, F32R = mybir.dt.float32, mybir.dt.float32r
ALU, ACT, AX = mybir.AluOpType, mybir.ActivationFunctionType, mybir.AxisListType


class Mark:

    def __init__(self, ctx, nc, stage, name, per_round, base):
        self.stage, self.name, self.per_round, self.sem = stage, name, per_round, ctx.enter_context(nc.semaphore(name))
        self.count, self.at, self.base = 0, {}, base
        stage.marks.append(self)

    def by(self, instruction, key=None, inc=1):
        instruction.then_inc(self.sem, inc)
        self.count += inc
        self.at[key] = self.count

    def wait(self, engine, rnd, key=None):
        engine.wait_ge(self.sem, rnd * self.per_round + (self.at[key] + self.base))

    def wait_all(self, engine, rnd):
        if not (isinstance(rnd, int) and rnd * self.per_round + self.count <= 0):
            engine.wait_ge(self.sem, rnd * self.per_round + (self.count + self.base))

    def wait_so_far(self, engine):
        self.wait_all(engine, self.stage.rnd)

    def wait_before(self, engine, rnd):
        if not (isinstance(rnd, int) and rnd <= 0):
            engine.wait_ge(self.sem, rnd * self.per_round + self.base)


class Stage:

    def __init__(self, ctx, nc, base=1):
        self.ctx, self.nc, self.marks, self.base, self.rnd = ctx, nc, [], base, 0

    def mark(self, name, per_round):
        return Mark(self.ctx, self.nc, self, name, per_round, self.base)

    def prime(self, engine):
        for s in self.marks:
            engine.sem_inc(s.sem, self.base)

    def start(self, rnd=0):
        self.rnd = rnd
        for s in self.marks:
            s.count = 0

    def end(self):
        wrong = [(s.name, s.per_round, s.count) for s in self.marks if s.count != s.per_round]
        assert not wrong, wrong


def merged(*lists):
    keyed = []
    for n, steps in enumerate(lists):
        total, done = sum(work for work, _ in steps), 0.0
        for i, (work, _) in enumerate(steps):
            keyed.append(((done + work / 2) / total, n, i))
            done += work
    return [lists[n][i][1] for _, n, i in sorted(keyed)]


LAG_VALUES, LAG_FINISH = 3, 5
HEAD_MAXIMA = 6
WAY_OF_MAXIMA = 12

REST = {
    "x_in": 30, "stats": 5, "ln_factors": 6.7, "xn": 3, "gate_top": 2, "gate_sum": 6, "picked": 4, "tree":
    15, "fk_hi": 2, "q_biased": 3, "q_square": 3, "q_rms": 27.1, "q_rope": 22.8, "q_parts": 10, "res_in":
    28, "tile_1": 10, "k_stack": 2, "q_stack": 2, "scores": 1, "last_max": 0.7, "max_parts": 8, "max_rows":
    15, "weights": 3.7, "weights_2": 7.6, "window": 28.8, "values": 2, "normalise": 0.5, "attn": 2.5,
    "attn_parts": 3.4
}
UNITS = [
    ("kvg", 0), ("q", 0), ("fk", 0), ("kvg", 1), ("fv", 0), ("qt", 0), ("q", 1), ("fk", 1),
    ("fv", 1), ("qt", 1), ("qt", 2), ("qt", 3)
]


class Order:

    def __init__(self, products=()):
        self.now, self.chains, self.products, self.begun = 0.0, [], deque(products), deque()

    def add(self, chain, after=0.0):
        self.chains.append([self.now + after, len(self.chains), chain])

    def run(self):
        while self.chains or self.products or self.begun:
            due = min((c for c in self.chains if c[2]), default=None)
            if due and due[0] <= self.now or not (self.products or self.begun):
                if due is None:
                    return
                self.now = max(self.now, due[0])
                work, rest = next(due[2], (None, None))
                if work is None:
                    due[2] = None
                    due[0] = float("inf")
                    if all(c[2] is None for c in self.chains):
                        self.chains = []
                else:
                    self.now += work
                    due[0] = self.now + rest
            else:
                if not self.begun:
                    self.begun.extend(self.products.popleft())
                work, step = self.begun.popleft()
                step()
                self.now += work


def mixed_attention_kernel(nc, x, w_tok, w_qt, w_o, b_qkv, b_o, w_norm, scale, rope, ident, rank, out):
    pe, dve, act, pool, sp = nc.tensor, nc.vector, nc.scalar, nc.gpsimd, nc.sync

    q_parts = nc.dram_tensor("q_parts", (2, DK, H, TOK), F32, kind="Internal").ap()
    partial = nc.dram_tensor("partial", (TOK, D), F32, kind="Internal").ap()

    top = ExitStack()

    def sb(ctx, name, shape, dt=F32):
        return ctx.enter_context(nc.sbuf_tensor(name, shape, dt))

    def pb(ctx, name, shape):
        return ctx.enter_context(nc.psum_tensor(name, shape, F32))

    idt = sb(top, "idt", [P, P])
    k_stack = sb(top, "k_stack", [P, TOK], F32R)
    v_all = sb(top, "v_all", [P, TILES, VW])

    one = ExitStack()
    w_tok_p = [sb(one, f"w_tok{n}", [P, KC, W_COLS], F32R) for n in range(2)]
    w_qt_p = [sb(one, f"w_qt{n}", [P, KC, HD], F32R) for n in range(2)]
    w_o_p = [sb(one, f"w_o{n}", [P, KC, D], F32R) for n in range(2)]
    cos_t = sb(one, "cos_t", [P, S // P, 2, DK])
    sin_t = sb(one, "sin_t", [P, S // P, 2, DK])
    bias = sb(one, "bias", [P, N_QKV])
    bias_o = sb(one, "bias_o", [P, D])
    rank_t = sb(one, "rank_t", [P, H])
    win_mask = sb(one, "win_mask", [P, 3 * HALF])
    k_win = sb(one, "k_win", [P, HKV, KEY0 + PAIR], F32R)
    q_win = [sb(one, f"q_win{a}", [P, H, P], F32R) for a in range(2)]
    v_nat = [sb(one, f"v_nat{a}", [P, HKV, VW]) for a in range(2)]
    v_shift = [sb(one, f"v_shift{a}", [P, HKV, VW]) for a in range(2)]
    key_bias = sb(one, "key_bias", [P, ROUNDS, 1])

    NH = H + HKV
    x_ln = sb(one, "x_ln", [P, 2, D])
    stats = sb(one, "stats", [P, 2, 6])
    moments = sb(one, "moments", [P, 2, 2])
    ln_v, ln_y, ln_t, ln_b = (sb(one, n, [P, 2]) for n in ("ln_v", "ln_y", "ln_t", "ln_b"))
    xt = [sb(one, f"xt{n}", [P, KC, PAIR], F32R) for n in range(2)]
    qt = [sb(one, f"qt{n}", [P, 2, PAIR], F32R) for n in range(2)]
    qkv = [sb(one, f"qkv{a}", [P, N_QKV]) for a in range(2)]
    rope_b = sb(one, "rope_b", [P, NH, DK])
    rope_sq = sb(one, "rope_sq", [P, NH, DK])
    rms_v, rms_y, rms_t = (sb(one, n, [P, NH]) for n in ("rms_v", "rms_y", "rms_t"))
    stack = [sb(one, f"stack{a}", [P, NH, HALVES]) for a in range(2)]
    picked = {k: sb(one, f"picked_{k}", [P, HD]) for k in ("fk", "fv")}
    fk_stack = [sb(one, f"fk_stack{a}", [P, HALVES]) for a in range(2)]
    g_max, g_sum, g_top, g_rank = (sb(one, n, [P, 2]) for n in ("g_max", "g_sum", "g_top", "g_rank"))
    g_exp, g_score, g_hot = (sb(one, n, [P, 2, H]) for n in ("g_exp", "g_score", "g_hot"))

    psum1 = ExitStack()
    gemm = [pb(psum1, f"gemm{n}", [P, 512]) for n in range(2)]
    tp1 = pb(psum1, "tp1", [P, 4, P])
    tp2 = pb(psum1, "tp2", [P, 4, P])
    s_win = [pb(psum1, f"s_win{n}", [P, 2, PAIR]) for n in range(2)]
    st_win = pb(psum1, "st_win", [P, 2, REP, HALF])
    ol = pb(psum1, "ol", [P, 2, REP, HALF])

    st0, st1, st2 = Stage(top, nc), Stage(top, nc), Stage(top, nc)
    x_in, xn_r = st0.mark("x_in", 16), st0.mark("xn_r", 2)
    ln_seq = st0.mark("ln_seq", 15)
    ln_b_r = st0.mark("ln_b_r", 1)
    seq = st1.mark("seq", 32)
    xt_mm, xt_hi, xt_lo = ([st.mark(f"{k}{a}", 1) for a, st in enumerate((st0, st1))]
                           for k in ("xt_mm", "xt_hi", "xt_lo"))
    gemm_mm, gemm_read = st1.mark("gemm_mm", 12), st1.mark("gemm_read", 12)
    kv_r, sq_r, rms_r = (st1.mark(n, 2) for n in ("kv_r", "sq_r", "rms_r"))
    rope_ab, rope_sum, rope_r, stack_hi, stack_r = (
        st1.mark(*a) for a in (("rope_ab", 8), ("rope_sum", 2), ("rope_r", 2), ("stack_hi", 6), ("stack_r", 2)))
    g_sum_r, g_top_r = (st1.mark(n, 2) for n in ("g_sum_r", "g_top_r"))
    tree = {k: st1.mark(f"tree_{k}", 8) for k in ("fk", "fv")}
    fk_hi, fk_lo, fk_dup, fv_out = (st1.mark(n, 2) for n in ("fk_hi", "fk_lo", "fk_dup", "fv_out"))
    qt_hi = st1.mark("qt_hi", 4)
    q_stored = [st1.mark(f"q_stored{c}", 64) for c in range(2)]
    fk_mm, fk_out = st2.mark("fk_mm", 1), st2.mark("fk_out", 1)
    v_old, v_r, k_old, k_mm, k_r = (st2.mark(n, k) for n, k in (
        ("v_old", 1), ("v_r", 5), ("k_old", 2), ("k_mm", 2), ("k_r", 2)))
    q_mm, q_r = st2.mark("q_mm", 8), st2.mark("q_r", 8)
    s_mm = [st2.mark(f"s_mm{n}", 8) for n in range(2)]
    s_max = [st2.mark(f"s_max{n}", 16) for n in range(2)]
    w_hi_r, w_lo_r, w_mm, w_t_r, w_in = (st2.mark(n, k) for n, k in (
        ("w_hi_r", 2), ("w_lo_r", 2), ("w_mm", 2), ("w_t_r", 2), ("w_in", 32)))
    st_mm, p_exp, p_low, p_r, pv_mm = (st2.mark(n, 8) for n in ("st_mm", "p_exp", "p_low", "p_r", "pv_mm"))
    o_r = st2.mark("o_r", 4)
    st3 = [Stage(top, nc) for a in range(2)]
    o_mm, rec_r, attn_r = ([st3[a].mark(f"{n}{a}", 2) for a in range(2)] for n in ("o_mm", "rec_r", "attn_r"))
    at_mm, at_hi, at_lo, wo_mm, res_bias, res_r = ([st3[a].mark(f"{n}{a}", 1) for a in range(2)] for n in (
        "at_mm", "at_hi", "at_lo", "wo_mm", "res_bias", "res_r"))
    res_in, res_stored = ([st3[a].mark(f"{n}{a}", 16) for a in range(2)] for n in ("res_in", "res_stored"))

    IT = S // P
    HG = HD // P
    HQ = H // HG
    ROUTED_SCALE = float(DK) ** -0.5
    stl, (sta, stb, fin) = [Stage(top, nc) for b in range(B)], (Stage(top, nc) for _ in range(3))
    out_done = [Stage(top, nc) for b in range(B)]
    q_in = [[stl[b].mark(f"q_in{b}{c}", 48) for c in range(4)] for b in range(B)]
    r_in = [stl[b].mark(f"r_in{b}", 16) for b in range(B)]
    rs_mm, rs_max = (sta.mark(n, IT * HQ) for n in ("rs_mm", "rs_max"))
    r_hi, r_lo, r_mm, r_t, r_row = (sta.mark(n, k) for n, k in (
        ("r_hi", 1), ("r_lo", 1), ("r_mm", 1), ("r_t", 1), ("r_row", 16)))
    PRODUCTS = [(i, j) for i in range(IT) for j in (i, *range(i))]
    RING = 6
    rst_mm, rp_exp, rpv = (stb.mark(n, len(PRODUCTS)) for n in ("rst_mm", "rp_exp", "rpv"))
    rp_diag = stb.mark("rp_diag", IT)
    ro_r, ro_mm, ro_rec, ro_norm, ro_out = (stb.mark(n, IT) for n in ("ro_r", "ro_mm", "ro_rec", "ro_norm", "ro_out"))
    stored = [out_done[b].mark(f"stored{b}", 16) for b in range(B)]
    masked = fin.mark("masked", 2)

    setup = Stage(top, nc, base=0)
    raw_used = [setup.mark(f"raw_used{n}", 3) for n in range(2)]
    raw_in = [setup.mark(f"raw_in{n}", 48) for n in range(2)]
    w_hi, const_in, filled, tables = (setup.mark(*a) for a in (
        ("w_hi", 6), ("const_in", 16 * 7), ("filled", 22), ("tables", 5)))
    primed = setup.mark("primed", 1)
    for stage in (st0, st1, st2, *st3, *stl, sta, stb, fin, *out_done):
        stage.prime(pool)
    primed.by(pool.memset(v_shift[0][:, 0, DK + 1:DK + 2], 0.0))

    over = ExitStack()
    raw = [sb(over, f"raw{n}", [P, KC, HD]) for n in range(2)]
    rope_t = sb(over, "rope_t", [P, S // P, 2, DK])
    norm_w = sb(over, "norm_w", [P, 2, 2, DK])
    scale_t = sb(over, "scale_t", [P, 1])

    def load_constants():
        const_in.by(act.dma_start(idt[:, :], ident), inc=16)
        const_in.by(act.dma_start(rope_t[:, :, :, :], rope.rearrange("(t p) a d -> p t a d", p=P)), inc=16)
        for dst, src in ((bias, b_qkv), (bias_o, b_o), (norm_w[:, :, :, :].rearrange("p a b d -> p (a b d)"), w_norm),
                         (scale_t, scale), (rank_t, rank)):
            dst = dst[:, :]
            const_in.by(act.dma_start(dst, src.to_broadcast(dst.shape)), inc=16)

    PIECES = [("kvg", w_tok, w_tok_p, C_KVG, C_FK - C_KVG), ("q", w_tok, w_tok_p, C_Q, HD),
              ("fk", w_tok, w_tok_p, C_FK, HD), ("fv", w_tok, w_tok_p, C_FV, HD), ("qt", w_qt, w_qt_p, 0, HD),
              ("wo", w_o, w_o_p, 0, D)]

    def load_piece(n):
        _, src, _, c0, cols = PIECES[n]
        raw_used[n % 2].wait_all(sp, 0)
        raw_in[n % 2].by(sp.dma_start(raw[n % 2][:, :, 0:cols],
                                      src[:, c0:c0 + cols].rearrange("(k p) c -> p k c", p=P)), n, inc=16)

    def piece_hi(n):
        _, _, dst, c0, cols = PIECES[n]
        raw_in[n % 2].wait(act, 0, n)
        w_hi.by(act.activation(dst[0][:, :, c0:c0 + cols], raw[n % 2][:, :, 0:cols], ACT.Copy), n)

    def piece_lo(n):
        _, _, dst, c0, cols = PIECES[n]
        w_hi.wait(dve, 0, n)
        raw_used[n % 2].by(dve.tensor_tensor(dst[1][:, :, c0:c0 + cols], raw[n % 2][:, :, 0:cols],
                                             dst[0][:, :, c0:c0 + cols].bitcast(F32), ALU.subtract), n)

    pieces_made = [0]

    def make_pieces(upto):
        while pieces_made[0] <= min(upto, len(PIECES) - 1):
            n = pieces_made[0]
            piece_hi(n)
            piece_lo(n)
            if n + 2 < len(PIECES):
                load_piece(n + 2)
            pieces_made[0] += 1

    def wait_for_piece(kind):
        n = [p[0] for p in PIECES].index(kind)
        make_pieces(n)
        raw_used[n % 2].wait(pe, 0, n)

    def make_tables():
        const_in.wait(dve, 0)
        tables.by(dve.tensor_scalar(norm_w[:, :, 0, :], norm_w[:, :, 0, :], scale_t[:, 0:1], None, ALU.mult))
        tables.wait(dve, 0)
        for part, table in ((0, cos_t), (1, sin_t)):
            for who in range(2):
                tables.by(dve.tensor_tensor(
                    table[:, :, who, :], rope_t[:, :, part, :],
                    norm_w[:, part, who, :].unsqueeze(1).to_broadcast([P, S // P, DK]), ALU.mult))


    def fill(instruction):
        filled.by(instruction)
        filled.wait(pool, 0)

    fill(pool.memset(v_all[:, :, :], 0.0))
    fill(pool.memset(v_all[:, :, DK:DK + 1], 1.0))
    filled.at["v_all"] = filled.count
    fill(pool.memset(k_stack[96:128, :].bitcast(F32), 1.0))
    fill(pool.memset(k_win[:, :, :].bitcast(F32), 0.0))
    fill(pool.memset(k_win[96:128, :, :].bitcast(F32), 1.0))
    fill(pool.memset(k_win[96:97, :, :].bitcast(F32), 0.0))
    for q in q_win:
        fill(pool.memset(q[96:128, :, :].bitcast(F32), 1.0))
    fill(pool.memset(key_bias[96:97, :, :], 0.0))
    for b in range(B):
        fill(pool.memset(key_bias[96:97, b * (S // PAIR):b * (S // PAIR) + 1, :], NEG))
    for v in (*v_nat, *v_shift):
        fill(pool.memset(v[:, :, :], 0.0))
        fill(pool.memset(v[:, :, DK:DK + 1], 1.0))
    fill(pool.memset(win_mask[:, :], 0.0))
    for sign in (1, -1):
        fill(pool.affine_select(out=win_mask[:, :], in_=win_mask[:, :], compare_op=ALU.is_ge, fill=NEG,
                                base=0 if sign == 1 else HALF, pattern=[[sign, 3 * HALF]],
                                channel_multiplier=-sign))

    def then(signal, instruction, engine, n, alone=False):
        signal.by(instruction, "last")
        signal.wait(engine, n, "last")
        if alone:
            stand_alone(engine)

    def stand_alone(engine):
        engine.nop(nofuse=True)

    def inv_sqrt(mark, v, y, t, n):
        i32 = mybir.dt.int32
        then(mark, dve.tensor_scalar(y.bitcast(i32), v.bitcast(i32), -0.5, float(0x5F3759DF), ALU.mult, ALU.add), dve, n)
        for step in range(3):
            then(mark, dve.tensor_tensor(t, y, y, ALU.mult), dve, n)
            then(mark, dve.scalar_tensor_tensor(t, t, -0.5, v, ALU.mult, ALU.mult), dve, n)
            last = dve.scalar_tensor_tensor(y, t, 1.5, y, ALU.add, ALU.mult)
            if step < 2:
                then(mark, last, dve, n)
        return last

    def layernorm(n):
        xt_mm[0].wait_before(sp, n)
        xt_mm[1].wait_before(sp, n)
        x_in.by(sp.dma_start(x_ln[:, :, :], x[bass.ds(n * PAIR, PAIR), :].rearrange("(a p) c -> p a c", p=P)), inc=16)
        yield 0, REST["x_in"]
        x_in.wait(dve, n)
        for a in range(2):
            ln_seq.by(dve.bn_stats(stats[:, a, :], x_ln[:, a, :]), a)
            yield 0, REST["stats"]
        for a in range(2):
            ln_seq.wait(dve, n, a)
            stand_alone(dve)
            ln_seq.by(dve.bn_aggr(moments[:, a, :], stats[:, a, :]), "moments")
        ln_seq.wait(dve, n, "moments")
        then(ln_seq, dve.tensor_scalar(ln_v[:, :], moments[:, :, 1], LN_EPS, None, ALU.add), dve, n)
        xn_r.wait_all(dve, n)
        then(ln_seq, inv_sqrt(ln_seq, ln_v[:, :], ln_y[:, :], ln_t[:, :], n), dve, n)
        ln_b_r.by(dve.scalar_tensor_tensor(ln_b[:, :], moments[:, :, 0], -1.0, ln_y[:, :], ALU.mult, ALU.mult))
        yield 0, REST["ln_factors"]
        ln_b_r.wait(act, n)
        for a in range(2):
            xn_r.by(act.activation(x_ln[:, a, :], x_ln[:, a, :], ACT.Identity, bias=ln_b[:, a:a + 1],
                                   scale=ln_y[:, a:a + 1]), a)
            yield 0, REST["xn"]

    def tp1_free():
        for s in (*xt_lo, fk_out):
            s.wait_so_far(pe)

    def transpose_x(n, a, now):
        xn_r.wait(pe, n, a)
        tp1_free()
        for kc in range(KC):
            i = pe.transpose(tp1[:, kc, :], x_ln[:, a, kc * P:(kc + 1) * P], idt[:, :])
        xt_mm[a].by(i, a)
        cols = slice(a * P, (a + 1) * P)
        if a:
            gemm_mm.wait_before(act, n)
        elif now >= 0 if isinstance(now, int) else True:
            gemm_mm.wait(act, now, UNITS[LAST_OF_0])
        xt_mm[a].wait(act, n, a)
        xt_hi[a].by(act.activation(xt[0][:, :, cols], tp1[:, :, :], ACT.Copy), a)
        xt_hi[a].wait(dve, n, a)
        xt_lo[a].by(dve.tensor_tensor(xt[1][:, :, cols], tp1[:, :, :], xt[0][:, :, cols].bitcast(F32), ALU.subtract), a)
        yield 3, 0

    LAST_OF_0 = UNITS.index(("qt", 3))
    COLS = {"q": (C_Q, HD), "kvg": (C_KVG, C_FK - C_KVG), "fk": (C_FK, HD), "fv": (C_FV, HD)}
    bank_free = [None, None]

    def take_bank(mark, rnd, key):
        bank, free = bank_free.pop(0)
        for wait in free:
            wait()
        bank_free.append((bank, [lambda: mark.wait(pe, rnd, key)]))
        return gemm[bank]

    def product(n, unit):
        kind, a = unit
        use = []

        def chunk(kc):
            if kc == 0:
                use.append(take_bank(gemm_read, n, unit))
                if isinstance(n, int) and n == 0:
                    wait_for_piece(kind)
                for t in ((0, 1) if kind == "qt" else (a,)):
                    xt_lo[t].wait(pe, n, t)
            g = use[0]
            for p, (l, r) in enumerate(((0, 0), (0, 1), (1, 0))):
                first, last = kc == 0 and p == 0, kc == KC - 1 and p == 2
                if kind == "qt":
                    i = pe.matmul(g[:, 0:PAIR], w_qt_p[r][:, kc, a * P:(a + 1) * P], xt[l][:, kc, :],
                                  start=first, stop=last)
                else:
                    c0, cols = COLS[kind]
                    i = pe.matmul(g[:, 0:cols], xt[l][:, kc, a * P:(a + 1) * P], w_tok_p[r][:, kc, c0:c0 + cols],
                                  start=first, stop=last)
            if kc == KC - 1 and isinstance(n, int) and n == 0:
                make_pieces(UNITS.index(unit) + 1)
            if kc == KC - 1:
                gemm_mm.by(i, unit)
                take = {"q": take_q, "kvg": take_kvg, "fk": take_routed, "fv": take_routed, "qt": take_qt}[kind]
                chain = take(n, kind, a, g)
                order[0].add(chain)

        work = 3 if kind in ("q", "fk", "fv") else 1.6
        return [(work, lambda kc=kc: chunk(kc)) for kc in range(KC)]

    def take_kvg(n, kind, a, g):
        kv = 2 * HKV * DK
        gate = g[:, kv:kv + H]
        gemm_mm.wait(dve, n, (kind, a))
        v_r.wait_before(dve, n)
        stack_hi.wait_before(dve, n)
        kv_r.by(dve.tensor_tensor(qkv[a][:, HD:N_QKV], g[:, 0:kv], bias[:, HD:N_QKV], ALU.add), a)
        then(seq, dve.tensor_reduce(g_max[:, a:a + 1], gate, AX.X, ALU.max), dve, n)
        seq.by(dve.scalar_tensor_tensor(g_score[:, a, :], gate, g_max[:, a:a + 1], rank_t[:, :],
                                        ALU.is_equal, ALU.mult), "last")
        gemm_read.by(dve.tensor_scalar(g_exp[:, a, :], gate, g_max[:, a:a + 1], None, ALU.subtract), (kind, a))
        yield 0, REST["gate_top"]
        seq.wait(dve, n, "last")
        then(seq, dve.tensor_reduce(g_rank[:, a:a + 1], g_score[:, a, :], AX.X, ALU.max), dve, n)
        then(seq, dve.tensor_scalar(g_hot[:, a, :], g_score[:, a, :], g_rank[:, a:a + 1], None, ALU.is_equal), dve, n)
        gemm_read.wait(act, n, (kind, a))
        g_sum_r.by(act.activation(g_exp[:, a, :], g_exp[:, a, :], ACT.Exp, accum_out=g_sum[:, a:a + 1]), a)
        yield 0, REST["gate_sum"]
        g_sum_r.wait(dve, n, a)
        fv_out.wait_all(dve, n)
        g_top_r.by(dve.reciprocal(g_top[:, a:a + 1], g_sum[:, a:a + 1]), a)

    def take_routed(n, kind, a, g):
        buf = picked[kind]
        gemm_mm.wait(dve, n, (kind, a))
        if kind == "fk":
            fk_dup.wait_all(dve, n)
            fk_lo.wait_all(dve, n)
        else:
            fv_out.wait_all(dve, n)
        gemm_read.by(dve.tensor_tensor(
            buf[:, :].rearrange("p (h d) -> p h d", h=H), g[:, :].rearrange("p (h d) -> p h d", h=H),
            g_hot[:, a, :].unsqueeze(2).to_broadcast([P, H, DK]), ALU.mult), (kind, a))
        yield 0, REST["picked"]
        gemm_read.wait(pool, n, (kind, a))
        w = HD // 2
        while w >= DK:
            tree[kind].by(pool.tensor_tensor(buf[:, 0:w], buf[:, 0:w], buf[:, w:2 * w], ALU.add), (a, w))
            if w > DK:
                tree[kind].wait(pool, n, (a, w))
            w //= 2
        yield 0, REST["tree"]
        tree[kind].wait(act, n, (a, DK))
        if kind == "fv":
            g_top_r.wait(act, n, a)
            fv_out.by(act.activation(v_all[:, bass.ds(2 * n + a, 1), 0:DK], buf[:, 0:DK].unsqueeze(1), ACT.Copy,
                                     scale=g_top[:, a:a + 1]), a)
            return
        fk_mm.wait_before(act, n)
        dst = fk_stack[a]
        fk_hi.by(act.activation(dst[:, 0:DK].bitcast(F32R), buf[:, 0:DK], ACT.Copy), a)
        fk_dup.by(act.activation(dst[:, DK:2 * DK].bitcast(F32R), buf[:, 0:DK], ACT.Copy), a)
        yield 0, REST["fk_hi"]
        fk_hi.wait(dve, n, a)
        fk_lo.by(dve.tensor_tensor(dst[:, 2 * DK:3 * DK].bitcast(F32R), buf[:, 0:DK], dst[:, 0:DK], ALU.subtract), a)

    def take_q(n, kind, a, g):
        gemm_mm.wait(dve, n, (kind, a))
        stack_hi.wait_before(dve, n)
        gemm_read.by(dve.tensor_tensor(qkv[a][:, 0:HD], g[:, :], bias[:, 0:HD], ALU.add), (kind, a))
        qk = qkv[a][:, 0:NH * DK].rearrange("p (h d) -> p h d", h=NH)
        yield 0, REST["q_biased"]
        gemm_read.wait(act, n, (kind, a))
        kv_r.wait(act, n, a)
        sq_r.by(act.activation(rope_sq[:, :, :], qk, ACT.Square), a)
        gemm_read.wait(pool, n, (kind, a))
        kv_r.wait(pool, n, a)
        rope_sum.wait_all(pool, n)
        if isinstance(n, int) and n == 0:
            tables.wait_all(pool, 0)
        t = bass.ds((2 * n + a) % (S // P), 1)
        both = ((1, H, HKV), (0, 0, H))
        for who, h0, hn in both:
            sin_w = sin_t[:, t, who, :].rearrange("p o (s d) -> p o s d", s=2).to_broadcast([P, hn, 2, DK // 2])
            rope_ab.by(pool.tensor_tensor(
                rope_b[:, h0:h0 + hn, :].rearrange("p h (s d) -> p h s d", s=2),
                qk[:, h0:h0 + hn, :].rearrange("p h (s d) -> p h s d", s=2)[:, :, ::-1, :], sin_w, ALU.mult), a)
        sq_r.wait(pool, n, a)
        rope_ab.wait(pool, n, a)
        for who, h0, hn in both:
            rope_ab.by(pool.tensor_tensor(qk[:, h0:h0 + hn, :], qk[:, h0:h0 + hn, :],
                                          cos_t[:, t, who, :].to_broadcast([P, hn, DK]), ALU.mult), a)
        yield 0, REST["q_square"]
        sq_r.wait(dve, n, a)
        then(seq, dve.tensor_reduce(rms_t[:, :], rope_sq[:, :, :], AX.X, ALU.add), dve, n)
        then(seq, dve.tensor_scalar(rms_v[:, :], rms_t[:, :], 1.0 / DK, RMS_EPS, ALU.mult, ALU.add), dve, n)
        rms_r.by(inv_sqrt(seq, rms_v[:, :], rms_y[:, :], rms_t[:, :], n), a)
        yield 0, REST["q_rms"]
        rope_ab.wait(dve, n, a)
        rope_sum.by(dve.tensor_tensor(qk, qk, rope_b[:, :, :], ALU.add), a)
        rope_sum.wait(dve, n, a)
        rms_r.wait(dve, n, a)
        rope_r.by(dve.tensor_tensor(qk, qk, rms_y[:, :].unsqueeze(2).to_broadcast([P, NH, DK]), ALU.mult), a)
        yield 0, REST["q_rope"]
        while st2_runs[0] and q_mm.count < HKV * (a + 1):
            yield 0, 1
        rope_r.wait(act, n, a)
        if not (isinstance(n, int) and n == 0):
            q_mm.wait(act, n - 1, (a, HKV - 1))
        st = stack[a]
        stack_hi.by(act.activation(st[:, :, 0:DK].bitcast(F32R), qk, ACT.Copy), (a, "hi"))
        for h0, h1, dup in ((0, H, 2), (H, NH, 1)):
            stack_hi.by(act.activation(st[:, h0:h1, dup * DK:(dup + 1) * DK].bitcast(F32R), qk[:, h0:h1, :],
                                       ACT.Copy), (a, "dup"))
        yield 0, REST["q_parts"]
        stack_hi.wait(dve, n, (a, "hi"))
        for h0, h1, lo in ((0, H, 1), (H, NH, 2)):
            i = dve.tensor_tensor(st[:, h0:h1, lo * DK:(lo + 1) * DK].bitcast(F32R), qk[:, h0:h1, :],
                                  st[:, h0:h1, 0:DK], ALU.subtract)
            (stack_r if h0 else seq).by(i, a)

    def take_qt(n, kind, c, g):
        q_stored[c % 2].wait_all(act, n)
        gemm_mm.wait(act, n, (kind, c))
        qt_hi.by(act.activation(qt[0][:, c % 2, :], g[:, 0:PAIR], ACT.Copy), c)
        qt_hi.wait(dve, n, c)
        gemm_read.by(dve.tensor_tensor(qt[1][:, c % 2, :], g[:, 0:PAIR], qt[0][:, c % 2, :].bitcast(F32),
                                       ALU.subtract), (kind, c))
        gemm_read.wait(sp, n, (kind, c))
        for part in range(2):
            dst = q_parts[part, :, 4 * c:4 * c + 4, bass.ds(n * PAIR, PAIR)].rearrange("d h t -> h d t")
            q_stored[c % 2].by(sp.dma_start(dst, qt[part][:, c % 2, :].bitcast(F32)), inc=16)
        yield 0, 0

    def load_old(m):
        kk = k_win[0:HALVES, :, HALF:KEY0]
        pv_mm.wait_all(act, m)
        v_old.by(act.activation(v_shift[0][0:HALF, :, 0:DK], v_nat[1][HALF:P, :, 0:DK], ACT.Copy))
        k_old.by(act.activation(kk, k_win[0:HALVES, :, PAIR + HALF:PAIR + KEY0].bitcast(F32), ACT.Copy))
        k_old.by(act.activation(k_win[96:97, :, HALF:KEY0], key_bias[96:97, bass.ds(m, 1), :].to_broadcast(
            [1, HKV, HALF]), ACT.Copy))
        v_old.wait(act, m)
        kv_r.wait(act, m, 1)
        val = [qkv[a][:, NH * DK:].rearrange("p (g d) -> p g d", g=HKV) for a in range(2)]
        v_r.by(act.activation(v_shift[1][0:HALF, :, 0:DK], val[0][HALF:P], ACT.Copy))
        for a in range(2):
            v_r.by(act.activation(v_shift[a][HALF:P, :, 0:DK], val[a][0:HALF], ACT.Copy))
            v_r.by(act.activation(v_nat[a][:, :, 0:DK], val[a], ACT.Copy))

    def load_res(m, a):
        res_stored[a].wait_all(sp, m)
        res_in[a].by(sp.dma_start(x_res[:, a, :], x[bass.ds(m * PAIR + a * P, P), :]), inc=16)
        yield 0, REST["res_in"]
        res_in[a].wait(pool, m)
        res_bias[a].by(pool.tensor_tensor(x_res[:, a, :], x_res[:, a, :], bias_o[:, :], ALU.add))

    def routed_key_stacks(m):
        fk_lo.wait(pe, m, 1)
        fk_dup.wait(pe, m, 1)
        tp1_free()
        for a in range(2):
            i = pe.transpose(tp1[0:HALVES, a, :], fk_stack[a][:, :], idt[:, :])
        fk_mm.by(i)
        fk_mm.wait(act, m)
        fk_out.by(act.activation(k_stack[0:HALVES, bass.ds(2 * m * P, PAIR)].rearrange("p (a t) -> p a t", a=2),
                                 tp1[0:HALVES, 0:2, :], ACT.Copy))

    def tp2_free():
        for s in (k_r, q_r, w_t_r, *at_lo):
            s.wait_so_far(pe)

    def key_stack(m, a):
        stack_r.wait(pe, m, a)
        stack_hi.wait(pe, m, (a, "dup"))
        tp2_free()
        for g in range(HKV):
            i = pe.transpose(tp2[0:HALVES, g, :], stack[a][:, H + g, :], idt[:, :])
        k_mm.by(i, a)
        k_mm.wait(act, m, a)
        k_old.wait(act, m)
        k_r.by(act.activation(k_win[0:HALVES, :, KEY0 + a * P:KEY0 + (a + 1) * P], tp2[0:HALVES, :, :], ACT.Copy), a)

    def query_stack(m, a, g):
        stack_r.wait(pe, m, a)
        stack_hi.wait(pe, m, (a, "dup"))
        tp2_free()
        for h in range(REP):
            i = pe.transpose(tp2[0:HALVES, h, :], stack[a][:, REP * g + h, :], idt[:, :])
        q_mm.by(i, (a, g))
        q_mm.wait(act, m, (a, g))
        st_mm.wait_before(act, m)
        q_r.by(act.activation(q_win[a][0:HALVES, REP * g:REP * g + REP, :], tp2[0:HALVES, :, :], ACT.Copy), (a, g))

    def s_win_free(n):
        for s in (s_max[n], *attn_r):
            s.wait_so_far(pe)

    def scores(m, a, g, pair):
        n = pair
        q_r.wait(pe, m, (a, g))
        k_r.wait(pe, m, a)
        s_win_free(n)
        for k in range(2):
            h = REP * g + 2 * pair + k
            i = pe.matmul(s_win[n][:, k, :], q_win[a][0:HALVES + 1, h, :], k_win[0:HALVES + 1, g, a * P:a * P + PAIR],
                          start=True, stop=True)
        s_mm[n].by(i, (a, g))
        s_mm[n].wait(dve, m, (a, g))
        if g == 0 and pair == 0:
            w_lo_r.wait_all(dve, m)
        stand_alone(dve)
        for k in range(2):
            h = REP * g + 2 * pair + k
            s_max[n].by(dve.tensor_tensor_reduce(
                out=s_win[n][:, k, HALF:PAIR], in0=s_win[n][:, k, HALF:PAIR], in1=win_mask[:, :], scale=1.0,
                scalar=NEG, op0=ALU.add, op1=ALU.max, accum_out=w_max[:, h:h + 1]), (a, g))

    def maxima(m, a):
        w_mm.wait_all(dve, m)
        for s in s_max:
            s.wait(dve, m, (a, HKV - 1))
        w_hi_r.by(dve.tensor_scalar(w_max_p[:, 0, :].bitcast(F32R), w_max[:, :], -1.0, None, ALU.mult), a)
        w_hi_r.wait(dve, m, a)
        w_lo_r.by(dve.scalar_tensor_tensor(w_max_p[:, 1, :].bitcast(F32R), w_max[:, :], -1.0, w_max_p[:, 0, :],
                                           ALU.mult, ALU.subtract), a)

    def maxima_rows(m, a):
        w_lo_r.wait(pe, m, a)
        tp2_free()
        w_mm.by(pe.transpose(tp2[0:2 * H, 0, :], w_max_p[:, :, :].rearrange("p s h -> p (s h)"), idt[:, :]), a)
        w_in.wait_all(act, m)
        w_mm.wait(act, m, a)
        w_t_r.by(act.activation(w_max_t[:, :], tp2[0:2 * H, 0, :], ACT.Copy), a)
        w_t_r.wait(sp, m, a)
        w_in.by(sp.dma_start(q_win[a][HALVES + 1:HALVES + 3, :, :].bitcast(F32),
                             w_max_t[:, :].bitcast(F32)), a, inc=16)

    def weights(m, a, blk, kvp):
        key, p_w = (a, blk, kvp), p_win[2 * blk + kvp]
        w_in.wait(pe, m, a)
        q_r.wait(pe, m, (a, HKV - 1))
        p_exp.wait_all(pe, m)
        w0 = HALF + a * P + blk * HALF
        for c in range(2):
            g = 2 * kvp + c
            i = pe.matmul(st_win[:, c, :, :], k_win[0:HALVES + 3, g, w0:w0 + P],
                          q_win[a][0:HALVES + 3, REP * g:REP * g + REP, blk * HALF:(blk + 1) * HALF], start=True, stop=True)
        st_mm.by(i, key)
        st_mm.wait(act, m, key)
        if a:
            pv_mm.wait(act, m, (0, blk, kvp))
        else:
            pv_mm.wait_before(act, m)
        p_exp.by(act.activation(p_w[:, :, :, :], st_win[:, :, :, :], ACT.Exp), key)

    def window(m, a, blk, kvp):
        key, p_w = (a, blk, kvp), p_win[2 * blk + kvp]
        p_exp.wait(pool, m, key)
        stand_alone(pool)
        for sign, s in ((1, p_low), (-1, p_r)):
            s.by(pool.affine_select(out=p_w[:, :, :, :], in_=p_w[:, :, :, :], compare_op=ALU.is_ge, fill=0.0,
                                    base=0 if sign == 1 else HALF, pattern=[[0, 2], [0, REP], [-sign, HALF]],
                                    channel_multiplier=sign), key)
            if s is p_low:
                s.wait(pool, m, key)
                stand_alone(pool)

    def values(m, a, blk, kvp):
        key = (a, blk, kvp)
        p_r.wait(pe, m, key)
        v_r.wait(pe, m)
        if kvp == 0:
            o_r.wait_all(pe, m)
        v = (v_nat if blk else v_shift)[a]
        for c in range(2):
            i = pe.matmul(ol[c * VW:(c + 1) * VW, kvp, :, :], v[:, 2 * kvp + c, :], p_win[2 * blk + kvp][:, c, :, :],
                          start=True, stop=True)
        pv_mm.by(i, key)
        if kvp == 1:
            pv_mm.wait(act, m, key)
            for s in o_mm:
                s.wait_so_far(act)
            o_r.by(act.activation(o_win[:, :, :, blk, :], ol[:, :, :, :], ACT.Copy), (a, blk))

    def normalise(m, a, kvp):
        o_r.wait(pe, m, (a, 1))
        s_win_free(kvp)
        for h in range(REP):
            i = pe.transpose(s_win[kvp][:, :, :].rearrange("p a (b c) -> p (a b) c", b=2)[:, h, :],
                             o_win[:, kvp, h, :, :].rearrange("p b q -> p (b q)"), idt[:, :])
        o_mm[a].by(i, kvp)
        o_mm[a].wait(dve, m, kvp)
        src = s_win[kvp][:, :, :].rearrange("p a b -> p (a b)").rearrange("p (h c v) -> p h c v", h=REP, c=2)
        rec_r[a].by(dve.reciprocal(recip[:, kvp, :, :], src[:, :, :, DK]), kvp)
        rec_r[a].wait(dve, m, kvp)
        for s in at_mm:
            s.wait_so_far(dve)
        dst = attn[:, kvp * 2 * REP * DK:(kvp + 1) * 2 * REP * DK].rearrange("p (c h d) -> p h c d", c=2, h=REP)
        attn_r[a].by(dve.tensor_tensor(dst, src[:, :, :, 0:DK],
                                    recip[:, kvp, :, :].unsqueeze(3).to_broadcast([P, REP, 2, DK]), ALU.mult), kvp)

    def attn_transposed(m, a):
        attn_r[a].wait(pe, m, 1)
        tp2_free()
        for kc in range(KC):
            i = pe.transpose(tp2[:, kc, :], attn[:, kc * P:(kc + 1) * P], idt[:, :])
        at_mm[a].by(i)
        at_mm[a].wait(act, m)
        for s in wo_mm:
            s.wait_so_far(act)
        at_hi[a].by(act.activation(attn_t[0][:, :, :], tp2[:, :, :], ACT.Copy))
        at_hi[a].wait(dve, m)
        at_lo[a].by(dve.tensor_tensor(attn_t[1][:, :, :], tp2[:, :, :], attn_t[0][:, :, :].bitcast(F32), ALU.subtract))

    def out_projection(m, a):
        use = []

        def chunk(kc):
            if kc == 0:
                use.append(take_bank(res_r[a], m, None))
                at_lo[a].wait(pe, m)
            for p, (l, r) in enumerate(((0, 0), (0, 1), (1, 0))):
                i = pe.matmul(use[0][:, :], attn_t[l][:, kc, :], w_o_p[r][:, kc, :], start=kc == 0 and p == 0,
                              stop=kc == KC - 1 and p == 2)
            if kc < KC - 1:
                return
            wo_mm[a].by(i)
            wo_mm[a].wait(dve, m)
            res_bias[a].wait(dve, m)
            res_r[a].by(dve.tensor_tensor(x_res[:, a, :], use[0][:, :], x_res[:, a, :], ALU.add))
            res_r[a].wait(sp, m)
            res_stored[a].by(sp.dma_start(partial[bass.ds(m * PAIR + a * P, P), :], x_res[:, a, :]), inc=16)

        return [(3, lambda kc=kc: chunk(kc)) for kc in range(KC)]

    def attend(m, a):
        if a == 0:
            load_old(m)
        key_stack(m, a)
        yield 3, REST["k_stack"]
        if a == 0:
            routed_key_stacks(m)
        for g in range(HKV):
            query_stack(m, a, g)
            yield 3, REST["q_stack"]
            if g:
                for k in range(2):
                    scores(m, a, g - 1, k)
                    yield 1, REST["scores"]
        for k in range(2):
            scores(m, a, HKV - 1, k)
            yield 1, REST["scores"]
        yield 0, REST["last_max"]
        maxima(m, a)
        if a == 0:
            order[0].add(attend(m, 1), REST["tile_1"])
        yield 0, REST["max_parts"]
        maxima_rows(m, a)
        yield 1, REST["max_rows"]
        for blk in range(2):
            for kvp in range(2):
                weights(m, a, blk, kvp)
                yield 2, REST["weights"]
                order[0].add(window_values(m, a, blk, kvp))
                yield 0, REST["weights_2"]

    def window_values(m, a, blk, kvp):
        window(m, a, blk, kvp)
        yield 0, REST["window"]
        values(m, a, blk, kvp)
        yield 2, REST["values"]
        if (a, blk, kvp) == (0, 1, 1):
            order[0].add(project_out(m, a))

    def project_out(m, a):
        for k in range(2):
            normalise(m, a, k)
            yield 3, REST["normalise"]
        yield 0, REST["attn"]
        attn_transposed(m, a)
        yield 3, REST["attn_parts"]
        order[0].products.appendleft(out_projection(m, a))

    def first_loads():
        load_piece(1)
        make_tables()
        filled.wait(act, 0, "v_all")
        const_in.wait_all(pe, 0)
        piece_hi(0)
        yield 0, 100
        piece_lo(0)
        load_piece(2)
        pieces_made[0] = 1

    def body(n, stages, norm=True):
        for stage, rnd in ((st0, n + 1), (st1, n), (st2, n - 1), (st3[0], n - 1), (st3[1], n - 2)):
            stage.start(min(rnd, ROUNDS) if isinstance(rnd, int) else rnd)
        bank_free[:] = [(b, [lambda: gemm_read.wait_before(pe, st1.rnd), lambda: res_r[0].wait_before(pe, st3[0].rnd),
                             lambda: res_r[1].wait_before(pe, st3[1].rnd)]) for b in range(2)]
        st2_runs[0] = 2 in stages
        units = [product(n, unit) for unit in UNITS] if 1 in stages else []
        if norm:
            def transpose_next():
                order[0].add(transpose_x(n + 1, 0, n))
            units[LAST_OF_0].append((0, transpose_next))
        order[0] = Order(units)
        if 1 in stages:
            order[0].add(transpose_x(n, 1, n))
        if 3 in stages:
            order[0].add(load_res(n - 2, 1))
            order[0].add(project_out(n - 2, 1))
        if 2 in stages:
            order[0].add(attend(n - 1, 0))
            order[0].add(load_res(n - 1, 0))
        if norm:
            order[0].add(layernorm(n + 1), 2)
        order[0].run()
        for stage, done in ((st0, norm), (st1, 1 in stages), (st2, 2 in stages), (st3[0], 2 in stages),
                            (st3[1], 3 in stages)):
            if done:
                stage.end()

    order, st2_runs = [Order()], [False]
    st0.start()
    load_constants()
    load_piece(0)
    for e in (pe, dve, act, pool, sp):
        primed.wait_all(e, 0)
    order[0].add(layernorm(0))
    order[0].add(first_loads(), 1)
    order[0].run()
    order[0].add(transpose_x(0, 0, -1))
    order[0].run()
    st0.end()
    body(0, (1,))
    make_pieces(len(PIECES))
    for e in (pe, dve, act, pool, sp):
        for s in (*raw_used, tables, filled, const_in, primed):
            s.wait_all(e, 0)
    setup.end()
    over.close()
    x_res = sb(one, "x_res", [P, 2, D])
    w_max = sb(one, "w_max", [P, H])
    w_max_p = sb(one, "w_max_p", [P, 2, H])
    w_max_t = sb(one, "w_max_t", [2 * H, P], F32R)
    p_win = [sb(one, f"p_win{n}", [P, 2, REP, HALF]) for n in range(4)]
    o_win = sb(one, "o_win", [P, 2, REP, 2, HALF])
    recip = sb(one, "recip", [P, 2, REP, 2])
    attn = sb(one, "attn", [P, HD])
    attn_t = [sb(one, f"attn_t{n}", [P, KC, P], F32R) for n in range(2)]
    body(1, (1, 2))
    with nc.Fori(2, ROUNDS - 1, 1) as n:
        body(n, (1, 2, 3))
    body(ROUNDS - 1, (1, 2, 3), norm=False)
    body(ROUNDS, (2, 3), norm=False)
    body(ROUNDS + 1, (3,), norm=False)
    for e in (pe, dve, act, pool, sp):
        for s in (*q_stored, gemm_read, fv_out, stack_r):
            s.wait_before(e, ROUNDS)
        for s in (fk_out, *res_stored, *res_r, p_r, o_r):
            s.wait_before(e, ROUNDS)
    psum1.close()
    one.close()

    two = ExitStack()
    q_op = [sb(two, f"q_op{b}", [P, HQ, S], F32R) for b in range(B)]
    p_t = [sb(two, f"p_t{n}", [P, HQ, P]) for n in range(RING)]
    causal = sb(two, "causal", [P, S])
    r_max = sb(two, "r_max", [P, HQ, IT])
    r_max_p = sb(two, "r_max_p", [P, 2, HQ, IT])
    r_max_t = sb(two, "r_max_t", [2 * HQ * IT, P], F32R)
    o_sb = [sb(two, f"o_sb{n}", [P, 2, P]) for n in range(2)]
    o_rec = sb(two, "o_rec", [P, 2, 2])
    o_norm = sb(two, "o_norm", [P, P])
    res = [sb(two, f"res{b}", [P, IT, P]) for b in range(B)]
    out_sb = [sb(two, f"out_sb{b}", [P, IT, P]) for b in range(B)]
    s_ps = [pb(two, f"s_ps{n}", [P, S]) for n in range(2)]
    st_ps = [pb(two, f"st_ps{n}", [P, HQ, P]) for n in range(2)]
    o_ps = pb(two, "o_ps", [P, 2, P])
    tp_ps = pb(two, "tp_ps", [P, 4, P])

    masked.by(pool.memset(causal[:, :], 0.0))
    masked.wait(pool, 0)
    masked.by(pool.affine_select(out=causal[:, S - P:S], in_=causal[:, S - P:S], compare_op=ALU.is_ge, fill=NEG,
                                 base=0, pattern=[[-1, P]], channel_multiplier=1))
    masked.wait(dve, 0)

    def load_queries(u, hg, b, c):
        t = slice(c * PAIR, (c + 1) * PAIR)
        for blk, part in ((0, 0), (1, 1), (2, 0)):
            q_in[b][c].by(sp.dma_start(
                q_op[b][blk * DK:(blk + 1) * DK, :, t].bitcast(F32),
                q_parts[part, :, bass.ds(hg * HQ, HQ), b * S + c * PAIR:b * S + (c + 1) * PAIR]), inc=16)

    def load_partial(u, hg, b):
        r_in[b].by(sp.dma_start(res[b][:, :, :], partial[b * S:(b + 1) * S, bass.ds(hg * P, P)].rearrange(
            "(i p) c -> p i c", p=P)), inc=16)

    def ends_row(k):
        return k + 1 == len(PRODUCTS) or PRODUCTS[k + 1][0] > PRODUCTS[k][0]

    def row_scores(u, hg, b, i, h):
        t = i * HQ + h
        n = t % 2
        if h == 0 and i % 2 == 0:
            q_in[b][i // 2].wait_before(pe, hg + 1)
        if t < 2:
            rs_max.wait_before(pe, u)
        else:
            rs_max.wait(pe, u, t - 2)
        width = (i + 1) * P
        for c0 in range(0, width, 512):
            cols = max(min(width - c0, 512), 2 * P)
            m = pe.matmul(s_ps[n][:, c0:c0 + cols], q_op[b][0:HALVES, h, i * P:(i + 1) * P],
                          k_stack[0:HALVES, b * S + c0:b * S + c0 + cols], start=True, stop=True)
        rs_mm.by(m, t)
        rs_mm.wait(dve, u, t)
        if t == 0:
            r_lo.wait_all(dve, u)
        stand_alone(dve)
        rs_max.by(dve.tensor_tensor_reduce(
            out=s_ps[n][:, 0:width], in0=s_ps[n][:, 0:width], in1=causal[:, S - width:S], scale=1.0, scalar=NEG,
            op0=ALU.add, op1=ALU.max, accum_out=r_max[:, h, i:i + 1]), t)

    def row_maxima(u, b):
        r_mm.wait_all(dve, u)
        rs_max.wait_all(dve, u)
        r_hi.by(dve.tensor_scalar(r_max_p[:, 0, :, :].bitcast(F32R), r_max[:, :, :], -1.0, None, ALU.mult))
        r_hi.wait(dve, u)
        r_lo.by(dve.scalar_tensor_tensor(r_max_p[:, 1, :, :].bitcast(F32R), r_max[:, :, :], -1.0, r_max_p[:, 0, :, :],
                                         ALU.mult, ALU.subtract))

    def tp_ps_free():
        for s in (r_t, ro_norm):
            s.wait_so_far(pe)

    def maxima_into_rows(u, b):
        r_lo.wait(pe, u)
        tp_ps_free()
        stand_alone(pe)
        r_mm.by(pe.transpose(tp_ps[0:2 * HQ * IT, 0, :], r_max_p[:, :, :, :].rearrange("p s h i -> p (s h i)"), idt[:, :]))
        r_mm.wait(act, u)
        r_row.wait_all(act, u)
        r_t.by(act.activation(r_max_t[:, :], tp_ps[0:2 * HQ * IT, 0, :], ACT.Copy))
        r_t.wait(act, u)
        r_row.by(act.dma_start(q_op[b][HALVES:HALVES + 2, :, :].bitcast(F32),
                               r_max_t[:, :].bitcast(F32)), inc=16)

    def key_scores(u, b, k):
        (i, j), n, p = PRODUCTS[k], k % 2, p_t[k % RING]
        if k == 0:
            r_row.wait_before(pe, u + 1)
        if k < 2:
            rp_exp.wait_before(pe, u)
        else:
            rp_exp.wait(pe, u, k - 2)
        rst_mm.by(pe.matmul(st_ps[n][:, :, :], k_stack[0:HALVES + 2, b * S + j * P:b * S + (j + 1) * P],
                            q_op[b][0:HALVES + 2, :, i * P:(i + 1) * P], start=True, stop=True), k)
        rst_mm.wait(act, u, k)
        if k < RING:
            rpv.wait_before(act, u)
        else:
            rpv.wait(act, u, k - RING)
        rp_exp.by(act.activation(p[:, :, :], st_ps[n][:, :, :], ACT.Exp, scale=ROUTED_SCALE), k)
        if i == j:
            rp_exp.wait(pool, u, k)
            stand_alone(pool)
            rp_diag.by(pool.affine_select(out=p[:, :, :], in_=p[:, :, :], compare_op=ALU.is_ge, fill=0.0,
                                          base=0, pattern=[[0, HQ], [1, P]], channel_multiplier=-1), i)

    def weighted_values(u, b, k):
        (i, j), p = PRODUCTS[k], p_t[k % RING]
        if i == j:
            rp_diag.wait(pe, u, i)
        else:
            rp_exp.wait(pe, u, k)
        if i == j:
            ro_r.wait_all(pe, u)
        for c in range(2):
            m = pe.matmul(o_ps[c * VW:(c + 1) * VW, :, :], v_all[:, b * IT + j, :], p[:, 2 * c:2 * c + 2, :],
                          start=i == j, stop=ends_row(k))
        rpv.by(m, k)
        if ends_row(k):
            rpv.wait(act, u, k)
            ro_mm.wait_all(act, u)
            ro_r.by(act.activation(o_sb[i % 2][:, :, :], o_ps[:, :, :], ACT.Copy), i)

    def finish_rows(u, hg, b, i):
        ro_r.wait(pe, u, i)
        tp_ps_free()
        for h in range(2):
            m = pe.transpose(tp_ps[:, h, :], o_sb[i % 2][:, h, :], idt[:, :])
        ro_mm.by(m, i)
        ro_mm.wait(dve, u, i)
        src = tp_ps[:, 0:2, :].rearrange("p h (c v) -> p h c v", c=2)
        ro_rec.by(dve.reciprocal(o_rec[:, :, :], src[:, :, :, DK]), i)
        ro_rec.wait(dve, u, i)
        ro_norm.by(dve.tensor_tensor(o_norm[:, :].rearrange("p (c h d) -> p h c d", c=2, h=2), src[:, :, :, 0:DK],
                                     o_rec[:, :, :].unsqueeze(3).to_broadcast([P, 2, 2, DK]), ALU.mult), i)
        ro_norm.wait(dve, u, i)
        if i == 0:
            r_in[b].wait_before(dve, hg + 1)
            stored[b].wait_before(dve, hg)
        ro_out.by(dve.tensor_tensor(out_sb[b][:, i, :], o_norm[:, :], res[b][:, i, :], ALU.add), i)

    def store(u, hg, b):
        ro_out.wait_all(sp, u)
        stand_alone(sp)
        stored[b].by(sp.dma_start(out[b * S:(b + 1) * S, bass.ds(hg * P, P)].rearrange("(i p) c -> p i c", p=P),
                               out_sb[b][:, :, :]), inc=16)

    def weights_and_values(unit, ahead):
        u, hg, b = unit
        n = len(PRODUCTS)
        steps = []
        for k in range(n + LAG_FINISH):
            if k == n:
                main, steps = steps, []
            if k < n:
                steps.append((1, lambda k=k: key_scores(u, b, k)))
            if LAG_VALUES <= k < n + LAG_VALUES:
                steps.append((2.2, lambda k=k - LAG_VALUES: weighted_values(u, b, k)))
            if k >= LAG_FINISH and ends_row(k - LAG_FINISH):
                i = PRODUCTS[k - LAG_FINISH][0]
                steps.append((1, lambda i=i: finish_rows(u, hg, b, i)))
                if ahead and i % 2:
                    def load(c=i // 2):
                        rst_mm.wait_all(sp, u)
                        stand_alone(sp)
                        load_queries(*ahead, c)
                    steps.append((0.01, load))

        def last():
            store(u, hg, b)
            if ahead:
                load_partial(*ahead)
                stl[b].end()
            stb.end()
        return main, steps + [(0.01, last)]

    def phase(now, before, ahead, ending=None, ending_ahead=None):
        a_steps, b_steps, tail = [], [], []
        if now:
            u, hg, b = now
            sta.start(u)
            a_steps = [(0.6 + 0.62 * (i + 1), lambda i=i, h=h: row_scores(u, hg, b, i, h))
                       for i in range(IT) for h in range(HQ)]
            a_steps += [(3, lambda: row_maxima(u, b)), (1, lambda: maxima_into_rows(u, b))]
            if before:
                a_steps.append((WAY_OF_MAXIMA, lambda: None))
        if ending:
            tail = weights_and_values(ending, ending_ahead)[1]
            head = HEAD_MAXIMA if now else 0
            for step in merged(*[s for s in (tail, a_steps[:head]) if s]):
                step()
            a_steps = a_steps[head:]
        if before:
            stb.start(before[0])
            if ahead:
                stl[before[2]].start()
            b_steps = weights_and_values(before, ahead)[0]
        for step in merged(*[s for s in (b_steps, a_steps) if s]):
            step()
        if now:
            sta.end()

    for b in range(B):
        stl[b].start()
        for c in range(4):
            load_queries(b, 0, b, c)
        load_partial(b, 0, b)
        stl[b].end()
    def unit(hg, b):
        return 2 * hg + b, hg, b

    phase(unit(0, 0), None, None)
    phase(unit(0, 1), unit(0, 0), unit(1, 0))
    phase(unit(1, 0), unit(0, 1), unit(1, 1), unit(0, 0), unit(1, 0))
    with nc.Fori(1, HG - 1, 1) as hg:
        phase(unit(hg, 1), unit(hg, 0), unit(hg + 1, 0), unit(hg - 1, 1), unit(hg, 1))
        phase(unit(hg + 1, 0), unit(hg, 1), unit(hg + 1, 1), unit(hg, 0), unit(hg + 1, 0))
    g = HG - 1
    phase(unit(g, 1), unit(g, 0), None, unit(g - 1, 1), unit(g, 1))
    phase(None, unit(g, 1), None, unit(g, 0), None)
    phase(None, None, None, unit(g, 1), None)
    for b in range(B):
        stored[b].wait_before(sp, HG)
    two.close()
    top.close()


def rope_table():
    import numpy as np
    inv = (np.float32(1.0) / np.float32(10000.0) ** (np.arange(0, DK, 2, dtype=np.float32) / np.float32(DK)))
    f = np.arange(S, dtype=np.float32)[:, None] * inv.astype(np.float32)[None, :]
    c, s = np.cos(f), np.sin(f)
    return np.stack([np.concatenate([c, c], 1), np.concatenate([-s, s], 1)], 1).astype(np.float32)


def kernel(**inputs):
    import numpy as np
    import concourse.bacc as bacc
    from concourse.bass_utils import run_bass_kernel_spmd

    a = {k: np.asarray(v) for k, v in inputs.items()}
    even_first = np.concatenate([np.arange(0, DK, 2), np.arange(1, DK, 2)])
    odd_first = np.concatenate([np.arange(1, DK, 2), np.arange(0, DK, 2)])

    def heads(w):
        return w.reshape(-1, DK, *w.shape[1:])[:, even_first].reshape(w.shape)

    wq, wk = heads(a["L0_attn_Wq"]), heads(a["L0_attn_Wk"])
    fq, fk, fv = np.split(a["L0_ffn_W_qkv"], 3, axis=0)
    qn, kn = a["L0_attn_qn_w"], a["L0_attn_kn_w"]
    arrays = {
        "x": a["L0_attn_x"].reshape(TOK, D),
        "w_tok": np.concatenate([wq, wk, a["L0_attn_Wv"], a["L0_ffn_W_gate"], fk, fv], 0).T,
        "w_qt": fq.T,
        "w_o": a["L0_attn_Wo"].T,
        "b_qkv": np.concatenate([heads(a["L0_attn_bq"]), heads(a["L0_attn_bk"]), a["L0_attn_bv"]])[None, :],
        "b_o": a["L0_attn_bo"][None, :],
        "w_norm": np.concatenate([qn[even_first], kn[even_first], qn[odd_first], kn[odd_first]])[None, :],
        "scale": a["L0_attn_scale"].reshape(1, 1),
        "rope": rope_table(),
        "ident": np.eye(P, dtype=np.float32),
        "rank": (H - np.arange(H, dtype=np.float32))[None, :],
    }
    arrays = {k: np.ascontiguousarray(v) for k, v in arrays.items()}
    nc = bacc.Bacc("TRN2", target_bir_lowering=False, num_devices=1)
    args = [nc.dram_tensor(k, v.shape, mybir.dt.from_np(v.dtype), kind="ExternalInput").ap() for k, v in arrays.items()]
    out = nc.dram_tensor("out", (TOK, D), F32, kind="ExternalOutput").ap()
    mixed_attention_kernel(nc, *args, out)
    r = run_bass_kernel_spmd(nc, [arrays], core_ids=[0])
    return r.results[0]["out"].reshape(B, S, D)
```
